# Optimizing a Trainium2 kernel written in Bass

```python
import numpy as np
import jax
import jax.numpy as jnp

def _softmax(x, axis=-1):
    return jax.nn.softmax(x, axis=axis)

def _gelu(x):
    return jax.nn.gelu(x, approximate=True)

def _silu(x):
    return jax.nn.silu(x)

def _sigmoid(x):
    return jax.nn.sigmoid(x)

def _layernorm(x, axis=-1, eps=1e-05):
    m = jnp.mean(x, axis=axis, keepdims=True)
    v = jnp.var(x, axis=axis, keepdims=True)
    return (x - m) / jnp.sqrt(v + eps)

def _scatter_add(tgt, idx, src, axis=0):
    return tgt.at[idx].add(src)

def _segment_sum(src, seg, n):
    return jax.ops.segment_sum(src, seg, n)
kernel_name = 'mk_xattn_ffn_d2_seqx_r4_ea1f86'

def setup_inputs(seed: int=0):
    np.random.seed(seed)
    _w = jnp.asarray

    def _rec_inputs():
        import jax
        import jax.numpy as jnp
        _rk = jax.random.key(seed)
        x = -0.000125 + 0.9999 * jax.random.normal(jax.random.fold_in(_rk, 1), (16, 256, 512), jnp.float32)
        _lenS = 256 - jax.random.randint(jax.random.fold_in(_rk, 7), (16,), 0, max(1, 256 // 4) + 1, jnp.int32)
        _lenS2 = 256 - jax.random.randint(jax.random.fold_in(_rk, 8), (16,), 0, max(1, 256 // 4) + 1, jnp.int32)
        _ctx_2048P = jax.random.normal(jax.random.fold_in(_rk, 11), (16, 16, 512), jnp.float32)
        _ctx_2048c = jax.random.dirichlet(jax.random.fold_in(_rk, 511), 0.3 * jnp.ones((16,), jnp.float32), (16, 256))
        _ctx_2048t = jnp.einsum('bsk,bkd->bsd', _ctx_2048c, _ctx_2048P)
        _ctx_2048t = _ctx_2048t * jax.lax.rsqrt(jnp.mean(jnp.square(_ctx_2048t)) + 1e-12) * 0.953939
        ctx_2048 = -1.52775e-05 + 0.999936 * (_ctx_2048t + 0.3 * jax.random.normal(jax.random.fold_in(_rk, 611), (16, 256, 512), jnp.float32))
        return (x, ctx_2048)
    x, ctx_2048 = _rec_inputs()

    def _L0_xattn_setup():
        import jax, jax.numpy as jnp
        import numpy as np
        B, DIM1, DIM2, LATENT, T = (16, 256, 256, 128, 512)
        LN_EPS = 1e-05
        key = jax.random.key(seed)
        ks = jax.random.split(key, 8)

        def xavier(k, shape):
            fan_out, fan_in = shape
            std = float(np.sqrt(2.0 / (fan_in + fan_out)))
            return jax.random.normal(k, shape, dtype=jnp.float32) * std
        return {'input1': jax.random.normal(ks[0], (B, DIM1, T), dtype=jnp.float32), 'input2': jax.random.normal(ks[1], (B, DIM2, T), dtype=jnp.float32), 'theta_w': xavier(ks[2], (LATENT, DIM2)), 'theta_b': jnp.zeros((LATENT,), jnp.float32), 'phi_w': xavier(ks[3], (LATENT, DIM1)), 'phi_b': jnp.zeros((LATENT,), jnp.float32), 'g_w': xavier(ks[4], (LATENT, DIM1)), 'g_b': jnp.zeros((LATENT,), jnp.float32), 'ln_gamma': jnp.ones((LATENT, T), jnp.float32), 'ln_beta': jnp.zeros((LATENT, T), jnp.float32), 'out_w': xavier(ks[5], (DIM2, LATENT)), 'out_b': jnp.zeros((DIM2,), jnp.float32)}
    _L0_xattn_all = _L0_xattn_setup()
    _L0_xattn_in = {k: v for k, v in _L0_xattn_all.items() if k in ('theta_w', 'theta_b', 'phi_w', 'phi_b', 'g_w', 'g_b', 'ln_gamma', 'ln_beta', 'out_w', 'out_b')}
    del _L0_xattn_all

    def _L0_ffn_setup():
        import jax, jax.numpy as jnp
        import numpy as np
        B, S, D_IN, D_OUT = (4, 512, 512, 512)
        E, R, TOP_K = (8, 8, 2)
        ALPHA = 16.0
        SCALE = ALPHA / R
        key = jax.random.key(seed)
        ks = jax.random.split(key, 6)
        x = jax.random.normal(ks[0], (B, S, D_IN), dtype=jnp.float32)
        W_base = jax.random.normal(ks[1], (D_OUT, D_IN), dtype=jnp.float32) / np.sqrt(D_IN)
        b_base = jax.random.normal(ks[2], (D_OUT,), dtype=jnp.float32) * 0.01
        W_router = jax.random.normal(ks[3], (E, D_IN), dtype=jnp.float32) / np.sqrt(D_IN)
        A_w = jax.random.normal(ks[4], (E, R, D_IN), dtype=jnp.float32) / np.sqrt(D_IN)
        B_w = jax.random.normal(ks[5], (E, D_OUT, R), dtype=jnp.float32) * 0.02
        return {'x': x, 'W_base': W_base, 'b_base': b_base, 'W_router': W_router, 'A_w': A_w, 'B_w': B_w}
    _L0_ffn_all = _L0_ffn_setup()
    _L0_ffn_in = {k: v for k, v in _L0_ffn_all.items() if k in ('W_base', 'b_base', 'W_router', 'A_w', 'B_w')}
    del _L0_ffn_all

    def _L1_xattn_setup():
        import jax, jax.numpy as jnp
        import numpy as np
        N_HEAD = 8
        key = jax.random.key(seed)
        k1, k2, k3 = jax.random.split(key, 3)
        B, D, L = (4, 256, 512)
        q = jax.random.normal(k1, (B, D, L), dtype=jnp.float32)
        k = jax.random.normal(k2, (B, D, L), dtype=jnp.float32)
        v = jax.random.normal(k3, (B, D, L), dtype=jnp.float32)
        gamma = jnp.ones((), dtype=jnp.float32)
        return {'q': q, 'k': k, 'v': v, 'gamma': gamma}
    _L1_xattn_all = _L1_xattn_setup()
    _L1_xattn_in = {k: v for k, v in _L1_xattn_all.items() if k in ('gamma',)}
    del _L1_xattn_all

    def _L1_ffn_setup():
        import jax, jax.numpy as jnp
        import numpy as np
        B, S, D = (2, 512, 512)
        E, I, TOPK = (64, 192, 8)
        M = B * S
        CAP = 2 * (M * TOPK) // E

        def _moe(x, router_weight, gate_proj, up_proj, down_proj):
            b, s, d = x.shape
            xf = x.reshape(-1, d)
            m = xf.shape[0]
            logits = xf @ router_weight
            probs = jax.nn.softmax(logits.astype(jnp.float32), axis=-1)
            topw, topi = jax.lax.top_k(probs, TOPK)
            topw = topw / topw.sum(axis=-1, keepdims=True)
            flat_e = topi.reshape(-1)
            flat_w = topw.reshape(-1).astype(x.dtype)
            order = jnp.argsort(flat_e)
            se = flat_e[order]
            tok = order // TOPK
            counts = jax.ops.segment_sum(jnp.ones_like(flat_e), flat_e, num_segments=E)
            starts = jnp.cumsum(counts) - counts
            pos = jnp.arange(m * TOPK) - starts[se]
            valid = pos < CAP
            posc = jnp.minimum(pos, CAP - 1)
            xe = jnp.zeros((E, CAP, d), x.dtype).at[se, pos].set(xf[tok], mode='drop')
            h = jax.nn.silu(jnp.einsum('ecd,edi->eci', xe, gate_proj)) * jnp.einsum('ecd,edi->eci', xe, up_proj)
            ye = jnp.einsum('eci,eid->ecd', h, down_proj)
            contrib = jnp.where(valid[:, None], ye[se, posc], 0.0) * flat_w[order][:, None]
            out = jnp.zeros((m, d), x.dtype).at[tok].add(contrib)
            return out.reshape(b, s, d)
        key = jax.random.key(seed)
        k0, k1, k2, k3, k4 = jax.random.split(key, 5)
        return {'x': jax.random.normal(k0, (B, S, D), jnp.float32), 'router_weight': jax.random.normal(k1, (D, E), jnp.float32) * 0.02, 'gate_proj': jax.random.normal(k2, (E, D, I), jnp.float32) * 0.02, 'up_proj': jax.random.normal(k3, (E, D, I), jnp.float32) * 0.02, 'down_proj': jax.random.normal(k4, (E, I, D), jnp.float32) * 0.02}
    _L1_ffn_all = _L1_ffn_setup()
    _L1_ffn_in = {k: v for k, v in _L1_ffn_all.items() if k in ('router_weight', 'gate_proj', 'up_proj', 'down_proj')}
    del _L1_ffn_all
    return {'x': x, 'ctx_2048': ctx_2048, 'L0_xattn_theta_w': _L0_xattn_in['theta_w'], 'L0_xattn_theta_b': _L0_xattn_in['theta_b'], 'L0_xattn_phi_w': _L0_xattn_in['phi_w'], 'L0_xattn_phi_b': _L0_xattn_in['phi_b'], 'L0_xattn_g_w': _L0_xattn_in['g_w'], 'L0_xattn_g_b': _L0_xattn_in['g_b'], 'L0_xattn_ln_gamma': _L0_xattn_in['ln_gamma'], 'L0_xattn_ln_beta': _L0_xattn_in['ln_beta'], 'L0_xattn_out_w': _L0_xattn_in['out_w'], 'L0_xattn_out_b': _L0_xattn_in['out_b'], 'L0_ffn_W_base': _L0_ffn_in['W_base'], 'L0_ffn_b_base': _L0_ffn_in['b_base'], 'L0_ffn_W_router': _L0_ffn_in['W_router'], 'L0_ffn_A_w': _L0_ffn_in['A_w'], 'L0_ffn_B_w': _L0_ffn_in['B_w'], 'L1_xattn_gamma': _L1_xattn_in['gamma'], 'L1_ffn_router_weight': _L1_ffn_in['router_weight'], 'L1_ffn_gate_proj': _L1_ffn_in['gate_proj'], 'L1_ffn_up_proj': _L1_ffn_in['up_proj'], 'L1_ffn_down_proj': _L1_ffn_in['down_proj']}

def reference(x, ctx_2048, L0_xattn_theta_w, L0_xattn_theta_b, L0_xattn_phi_w, L0_xattn_phi_b, L0_xattn_g_w, L0_xattn_g_b, L0_xattn_ln_gamma, L0_xattn_ln_beta, L0_xattn_out_w, L0_xattn_out_b, L0_ffn_W_base, L0_ffn_b_base, L0_ffn_W_router, L0_ffn_A_w, L0_ffn_B_w, L1_xattn_gamma, L1_ffn_router_weight, L1_ffn_gate_proj, L1_ffn_up_proj, L1_ffn_down_proj):
    import jax
    import jax.numpy as jnp

    def _L0_xattn_ref(input1, input2, theta_w, theta_b, phi_w, phi_b, g_w, g_b, ln_gamma, ln_beta, out_w, out_b):
        import jax, jax.numpy as jnp
        import numpy as np
        B, DIM1, DIM2, LATENT, T = (16, 256, 256, 128, 512)
        LN_EPS = 1e-05
        theta_x = jnp.einsum('ld,bdt->btl', theta_w, input2) + theta_b
        phi_x = jnp.einsum('ld,bdt->blt', phi_w, input1) + phi_b[:, None]
        scores = jnp.einsum('btl,bls->bts', theta_x, phi_x)
        p = jax.nn.softmax(scores, axis=-1)
        g_x = jnp.einsum('ld,bdt->btl', g_w, input1) + g_b
        t_x = jnp.einsum('bts,bsl->blt', p, g_x)
        mu = jnp.mean(t_x, axis=(1, 2), keepdims=True)
        var = jnp.var(t_x, axis=(1, 2), keepdims=True)
        h = (t_x - mu) * jax.lax.rsqrt(var + LN_EPS) * ln_gamma + ln_beta
        h = jax.nn.relu(h)
        w_t = jnp.einsum('ol,blt->bot', out_w, h) + out_b[None, :, None]
        return w_t + input2

    def _L0_ffn_ref(x, W_base, b_base, W_router, A_w, B_w):
        import jax, jax.numpy as jnp
        import numpy as np
        B, S, D_IN, D_OUT = (4, 512, 512, 512)
        E, R, TOP_K = (8, 8, 2)
        ALPHA = 16.0
        SCALE = ALPHA / R
        y = jnp.einsum('bsd,od->bso', x, W_base) + b_base
        logits = jnp.einsum('bsd,ed->bse', x, W_router)
        topk_vals, topk_idx = jax.lax.top_k(logits, TOP_K)
        gates = jax.nn.softmax(topk_vals, axis=-1)
        h = jnp.einsum('bsd,erd->bser', x, A_w)
        expert_outs = jnp.einsum('bser,eor->bseo', h, B_w) * SCALE
        topk_outs = jnp.take_along_axis(expert_outs, topk_idx[..., None], axis=2)
        fused = jnp.sum(topk_outs * gates[..., None], axis=2)
        return y + fused

    def _L1_xattn_ref(q, k, v, gamma):
        import jax, jax.numpy as jnp
        import numpy as np
        N_HEAD = 8
        B, Dq, Lq = q.shape
        Dv, Lk = (v.shape[-2], v.shape[-1])
        h = N_HEAD
        dq = Dq // h
        dv = Dv // h
        qh = q.reshape(B, h, dq, Lq)
        kh = k.reshape(B, h, dq, Lk)
        vh = v.reshape(B, h, dv, Lk)
        scale = 1.0 / jnp.sqrt(jnp.asarray(dq, dtype=q.dtype))
        qk = jnp.einsum('bhdq,bhdl->bhql', qh, kh) * scale
        sm = jax.nn.softmax(qk, axis=-1)
        ret = jnp.einsum('bhql,bhdl->bhdq', sm, vh)
        ret = ret.reshape(B, Dv, Lq)
        return gamma * ret

    def _L1_ffn_ref(x, router_weight, gate_proj, up_proj, down_proj):
        import jax, jax.numpy as jnp
        import numpy as np
        B, S, D = (2, 512, 512)
        E, I, TOPK = (64, 192, 8)
        M = B * S
        CAP = 2 * (M * TOPK) // E

        def _moe(x, router_weight, gate_proj, up_proj, down_proj):
            b, s, d = x.shape
            xf = x.reshape(-1, d)
            m = xf.shape[0]
            logits = xf @ router_weight
            probs = jax.nn.softmax(logits.astype(jnp.float32), axis=-1)
            topw, topi = jax.lax.top_k(probs, TOPK)
            topw = topw / topw.sum(axis=-1, keepdims=True)
            flat_e = topi.reshape(-1)
            flat_w = topw.reshape(-1).astype(x.dtype)
            order = jnp.argsort(flat_e)
            se = flat_e[order]
            tok = order // TOPK
            counts = jax.ops.segment_sum(jnp.ones_like(flat_e), flat_e, num_segments=E)
            starts = jnp.cumsum(counts) - counts
            pos = jnp.arange(m * TOPK) - starts[se]
            valid = pos < CAP
            posc = jnp.minimum(pos, CAP - 1)
            xe = jnp.zeros((E, CAP, d), x.dtype).at[se, pos].set(xf[tok], mode='drop')
            h = jax.nn.silu(jnp.einsum('ecd,edi->eci', xe, gate_proj)) * jnp.einsum('ecd,edi->eci', xe, up_proj)
            ye = jnp.einsum('eci,eid->ecd', h, down_proj)
            contrib = jnp.where(valid[:, None], ye[se, posc], 0.0) * flat_w[order][:, None]
            out = jnp.zeros((m, d), x.dtype).at[tok].add(contrib)
            return out.reshape(b, s, d)
        return _moe(x, router_weight, gate_proj, up_proj, down_proj)
    x = x + _L0_xattn_ref(_layernorm(x, axis=-1), ctx_2048, L0_xattn_theta_w, L0_xattn_theta_b, L0_xattn_phi_w, L0_xattn_phi_b, L0_xattn_g_w, L0_xattn_g_b, L0_xattn_ln_gamma, L0_xattn_ln_beta, L0_xattn_out_w, L0_xattn_out_b)
    x = x + _L0_ffn_ref(_layernorm(x, axis=-1), L0_ffn_W_base, L0_ffn_b_base, L0_ffn_W_router, L0_ffn_A_w, L0_ffn_B_w)
    x = x + _L1_xattn_ref(_layernorm(x, axis=-1), ctx_2048, ctx_2048, L1_xattn_gamma)
    x = x + _L1_ffn_ref(_layernorm(x, axis=-1), L1_ffn_router_weight, L1_ffn_gate_proj, L1_ffn_up_proj, L1_ffn_down_proj)
    return x

_drawn_inputs = setup_inputs


def setup_inputs(seed=0):
    import zlib

    import numpy as np

    out = dict(_drawn_inputs(seed))
    spreads = {'L0_xattn_theta_b': (0.0, 0.1),
     'L0_xattn_phi_b': (0.0, 2.0),
     'L0_xattn_g_b': (0.0, 0.29),
     'L0_xattn_ln_gamma': (1.0, 0.2),
     'L0_xattn_ln_beta': (0.0, 0.1),
     'L0_xattn_out_b': (0.0, 0.8)}
    factors = {'L0_ffn_b_base': 7.166,
     'L1_ffn_router_weight': 8.0,
     'L1_ffn_gate_proj': 8.0,
     'L1_ffn_up_proj': 8.0,
     'L1_ffn_down_proj': 8.0}
    for name, (base, spread) in spreads.items():
        noise = np.random.default_rng([zlib.crc32(name.encode()), seed]).standard_normal(out[name].shape)
        drawn = base * np.exp(spread * noise) if base else spread * noise
        out[name] = jnp.asarray(drawn.astype(out[name].dtype))
    for name, factor in factors.items():
        out[name] = (out[name] * factor).astype(out[name].dtype)
    return out
```

```python
from contextlib import ExitStack

import numpy as np

import concourse.bass as bass
from concourse import mybir

ALU = mybir.AluOpType
ACT = mybir.ActivationFunctionType
X = mybir.AxisListType.X
F32 = mybir.dt.float32
F32R = mybir.dt.float32r
I32 = mybir.dt.int32
U32 = mybir.dt.uint32

P = 128
EPS = 1e-5


class Step:

    def __init__(self, line, run):
        self.line, self.run, self.waited, self.count = line, run, False, None


class Line:

    def __init__(self, sem):
        self.sem, self.items = sem, []

    def wait(self, *steps):
        for s in steps:
            if s is not None:
                s.waited = True
                self.items.append(("wait", s))

    def do(self, run, *after):
        self.wait(*after)
        self.last = Step(self, run)
        self.items.append(("do", self.last))
        return self.last

    def dma(self, run, done, *after):
        self.wait(*after)
        mark = done.next()
        self.items.append(("dma", (run, done.sem)))
        return mark

    def number(self):
        n = 0
        for kind, s in self.items:
            if kind == "do" and s.waited:
                n += 1
                s.count = n

    def play(self, engine):
        reached = {}
        for kind, s in self.items:
            if kind == "wait":
                sem, count = (s.line.sem, s.count) if isinstance(s, Step) else (s.sem, s.count)
                if reached.get(id(sem), 0) < count:
                    engine.wait_ge(sem, count)
                    reached[id(sem)] = count
            elif kind == "do":
                ins = s.run(engine)
                if s.waited:
                    ins.then_inc(self.sem, 1)
            else:
                s[0](engine).then_inc(s[1], 16)


class Mark:
    def __init__(self, sem, count):
        self.sem, self.count, self.waited = sem, count, True


class Arrivals:

    def __init__(self, sem):
        self.sem, self.count = sem, 0

    def next(self):
        self.count += 16
        return Mark(self.sem, self.count)


class Bank:

    def __init__(self, ap):
        self.ap, self.free = ap, []


class Ring:
    def __init__(self, banks):
        self.banks, self.n = banks, 0

    def take(self):
        self.n += 1
        return self.banks[(self.n - 1) % len(self.banks)]


def build(nc, a, out, slots_dram, dims):
    B, HALF, T, L, NHEAD, DQ, NE, NEXP, CAP, TOPK, NRANK = (
        dims[k] for k in ("B", "HALF", "T", "L", "NHEAD", "DQ", "NE", "NEXP", "CAP", "TOPK", "NRANK"))
    C = T // P
    NR = NE * NRANK
    NF = NR + 1
    ROWS = B * HALF * P
    INNER = dims["INNER"]
    IC = INNER // 2
    ROW = T + 1 + NEXP
    NSLOT = NEXP * CAP
    SCALE = float(DQ) ** -0.5
    SK = 3 * DQ
    SKM = SK + 2
    HPH = NHEAD // HALF

    stack = ExitStack()
    with stack:
        def sem(name):
            return stack.enter_context(nc.semaphore(name))

        def sb(name, shape, dt=F32, on=stack):
            return on.enter_context(nc.sbuf_tensor(name, shape, dt))

        PE, DVE, ACTE, POOL, SP = (Line(sem(n)) for n in ("pe_done", "dve_done", "act_done", "pool_done", "sp_done"))

        def arrivals(name):
            return Arrivals(sem(name))

        psum = [stack.enter_context(nc.psum_tensor(f"bank{i}", [P, 512], F32)) for i in range(8)]
        banks = [Bank(t) for t in psum]

        def mm(bank_ap, lhsT, rhs, start, stop, *after):
            return PE.do(lambda e: e.matmul(bank_ap, lhsT, rhs, start=start, stop=stop), *after)

        def tr(bank_ap, src, ident_ap, *after):
            return PE.do(lambda e: e.transpose(bank_ap, src, ident_ap), *after)

        small = ExitStack()
        stack.enter_context(small)
        ident = sb("ident", [P, P])
        ones = sb("ones", [P, P])

        def A(name, shape, dt=F32):
            return sb(name, shape, dt, small)

        below = A("below", [P, P])
        mean_w = A("mean_w", [P, P])
        neg_half = A("neg_half", [P, 2])
        iota8 = A("iota8", [P, NE])
        expert_off = A("expert_off", [P, NEXP])
        row_no = A("row_no", [P, 2])
        theta_w = A("theta_w", [P, HALF, L])
        phi_w = A("phi_w", [P, HALF, L])
        g_w = A("g_w", [P, HALF, L])
        lat_b = A("lat_b", [P, 3])
        ln_gamma = A("ln_gamma", [P, T])
        ln_beta = A("ln_beta", [P, T])
        out_w = A("out_w", [P, HALF * P])
        out_b = A("out_b", [P, HALF])
        base_w = A("base_w", [P, C, T])
        lora_in = A("lora_in", [P, C, NE + NR])
        lora_out = A("lora_out", [NF, T])
        route_w = A("route_w", [P, C, NEXP])
        gamma1 = A("gamma1", [P, 1])
        fill_row = A("fill_row", [P, 2, ROW])

        weights_in = arrivals("weights_in")

        def load(dst, src):
            return SP.dma(lambda e: e.dma_start(dst, src), weights_in)

        x_buf = [A(f"x{i}", [P, HALF, T]) for i in range(3)]
        ctx_buf = [A(f"ctx{i}", [P, HALF, T]) for i in range(2)]
        x_in = [arrivals(f"x_in{i}") for i in range(3)]
        ctx_in = [arrivals(f"ctx_in{i}") for i in range(2)]
        x_free, ctx_free = [[], [], []], [[], []]
        loaded = {}

        def load_batch(b):
            xb, cb = x_buf[b % 3], ctx_buf[b % 2]
            mx = SP.dma(lambda e: e.dma_start(xb[:, :, :], a["x"][b].rearrange("(h p) t -> p h t", p=P)),
                        x_in[b % 3], *x_free[b % 3])
            mc = SP.dma(lambda e: e.dma_start(cb[:, :, :], a["ctx"][b].rearrange("(h p) t -> p h t", p=P)),
                        ctx_in[b % 2], *ctx_free[b % 2])
            loaded[b] = (mx, mc)

        load_batch(0)
        for h in range(HALF):
            load(theta_w[:, h, :], a["theta_wT"][h * P:(h + 1) * P, :])
            load(phi_w[:, h, :], a["phi_wT"][h * P:(h + 1) * P, :])
            load(g_w[:, h, :], a["g_wT"][h * P:(h + 1) * P, :])
        load(lat_b[:, :], a["lat_b"])
        load(ln_gamma[:, :], a["ln_gamma"])
        load(ln_beta[:, :], a["ln_beta"])
        load(out_w[:, :], a["out_wT"])
        load(out_b[:, :], a["out_b"])
        load(base_w[:, :, :], a["base_wT"].rearrange("(c p) o -> p c o", p=P))
        load(lora_in[:, :, :], a["lora_in"].rearrange("(c p) o -> p c o", p=P))
        load(lora_out[:, :], a["lora_out"])
        load(route_w[:, :, :], a["route_w"].rearrange("(c p) o -> p c o", p=P))
        weights_ready = load(gamma1[:, :], a["gamma1"])

        q_st = [A(f"q_stack{i}", [SKM, NHEAD, T], F32R) for i in range(2)]
        k_st = [A(f"k_stack{i}", [SKM, NHEAD, T], F32R) for i in range(2)]
        v_t = [A(f"v_t{i}", [P, C, NHEAD, 2 * DQ]) for i in range(2)]
        max_col = [A(f"max_col{i}", [P, C, SKM]) for i in range(2)]

        m0 = POOL.do(lambda e: e.memset(ident[:, :], 0.0))
        ident_ok = POOL.do(lambda e: e.affine_select(out=ident[:, :], in_=ident[:, :], compare_op=ALU.not_equal,
                                                     fill=1.0, base=0, pattern=[[-1, P]], channel_multiplier=1), m0)
        ones_ok = POOL.do(lambda e: e.memset(ones[:, :], 1.0))
        mw_ok = POOL.do(lambda e: e.memset(mean_w[:, :], 1.0 / P))
        below_ok = POOL.do(lambda e: e.affine_select(out=below[:, :], in_=ones[:, :], compare_op=ALU.is_gt, fill=0.0,
                                                     base=0, pattern=[[1, P]], channel_multiplier=-1), ones_ok)
        POOL.do(lambda e: e.memset(neg_half[:, :], -0.5))
        POOL.do(lambda e: e.iota(iota8[:, :], pattern=[[1, NE]], base=0, channel_multiplier=0,
                                 allow_small_or_imprecise_dtypes=True))
        POOL.do(lambda e: e.iota(expert_off[:, :], pattern=[[CAP, NEXP]], base=1, channel_multiplier=0,
                                 allow_small_or_imprecise_dtypes=True))
        f0 = POOL.do(lambda e: e.memset(fill_row[:, :, :], 0.0))
        for c in range(2):
            dst = fill_row[:, c, T:T + 1].bitcast(I32)
            fill_ok = POOL.do(lambda e, d=dst, c=c: e.iota(d, pattern=[[0, 1]], base=ROWS + c * P,
                                                           channel_multiplier=1), f0)
        rn = POOL.do(lambda e: e.iota(row_no[:, :], pattern=[[P, 2]], base=0, channel_multiplier=1,
                                      allow_small_or_imprecise_dtypes=True))
        for i in range(2):
            POOL.do(lambda e, t=max_col[i]: e.memset(t[:, :, :], 0.0))
            consts_ok2 = POOL.do(lambda e, t=v_t[i]: e.memset(t[:, :, :, :], 1.0))
            consts_ok = DVE.do(lambda e, t=k_st[i]: e.memset(t[SK:SKM, :, :].bitcast(F32), 1.0))

        slots_filled = arrivals("slots_filled")
        EG = NEXP // 4
        for g in range(4):
            dst = slots_dram[g * EG * CAP:(g + 1) * EG * CAP, :].rearrange("(e c p) w -> p e c w", c=2, p=P)
            for e_ in range(EG):
                d = slots_dram[(g * EG + e_) * CAP:(g * EG + e_ + 1) * CAP, :].rearrange("(c p) w -> p c w", p=P)
                fm = SP.dma(lambda e, d=d: e.dma_start(d, fill_row[:, :, :]), slots_filled, fill_ok, f0)
        spare = out[ROWS:ROWS + CAP, :].rearrange("(c p) t -> p c t", p=P)
        fill_mark = SP.dma(lambda e: e.dma_start(spare, fill_row[:, :, 0:T]), slots_filled)

        xn = A("xn", [P, HALF, T])
        theta = A("theta", [P, T])
        phi = A("phi", [P, T])
        g_sb = A("g_sb", [P, T])
        prob = A("prob", [P, C, T])
        prob_t = A("prob_t", [P, C, T])
        lat = A("lat", [P, T])
        res = A("res", [P, T])
        x_t = A("x_t", [P, C, P])
        x_t2 = A("x_t2", [P, C, P])
        hi = A("hi", [P, HALF, T], F32R)
        lo = A("lo", [P, HALF, T], F32R)
        stat = A("stat", [P, 2, 6])
        mv = A("mv", [P, 2, 2])
        rstd = A("rstd", [P, 2])
        stat4 = A("stat4", [P, 2, 6])
        mv4 = A("mv4", [P, 2, 2])
        rstd4 = A("rstd4", [P, 2])
        lst = A("lst", [P, 6])
        lmv = A("lmv", [P, 2])
        lmo = A("lmo", [P, 2])
        ltot = A("ltot", [P, 4])
        nmax1 = A("nmax1", [P, C])
        sum1 = A("sum1", [P, C])
        rl = A("rl", [P, NE + NR])
        top2 = A("top2", [P, 8])
        top2i = A("top2i", [P, 8], U32)
        top2f = A("top2f", [P, 2])
        gsc = A("gsc", [P, 8])
        gate = A("gate", [P, 2, NE])
        gated = A("gated", [P, NF])
        gated_t = A("gated_t", [NF, P])
        p_t = [A(f"p_t{i}", [P, T]) for i in range(4)]
        mx = [A(f"mx{i}", [P, C]) for i in range(2)]
        rec = [A(f"rec{i}", [P, T]) for i in range(2)]
        att = [A(f"att{i}", [P, T]) for i in range(2)]
        row = [A(f"row{i}", [P, ROW]) for i in range(2)]
        rt = A("rt", [P, 8])
        ex = A("ex", [P, NEXP])
        pr = A("pr", [P, NEXP])
        top8 = A("top8", [P, 8])
        repl = A("repl", [P, NEXP])
        mask = A("mask", [P, NEXP])
        seen = A("seen", [P, NEXP])
        over = A("over", [P, NEXP])
        grid = A("grid", [P, NEXP])
        slot8 = A("slot8", [P, 8])
        slot_i = [A(f"slot_i{i}", [P, 8], I32) for i in range(2)]

        gated_one = DVE.do(lambda e: e.memset(gated[:, :], 1.0))
        seen_ok = DVE.do(lambda e: e.memset(seen[:, :], 0.0))
        for line in (PE, ACTE, DVE, POOL):
            line.wait(weights_ready, consts_ok, consts_ok2, ident_ok, below_ok, mw_ok, rn, gated_one, seen_ok)

        misc = Ring(banks[6:8])

        def norm_rows(src, dst, st, m, r, ready, dst_free):
            n = len(src)
            for i in range(n):
                s = DVE.do(lambda e, i=i: e.bn_stats(st[:, i, :], src[i]), *ready)
                agg = DVE.do(lambda e, i=i: e.bn_aggr(m[:, i, :], st[:, i, :]), s)
            v = POOL.do(lambda e: e.tensor_scalar(r[:, 0:n], m[:, 0:n, 1], EPS, None, ALU.add), agg)
            w = POOL.do(lambda e: e.tensor_tensor(r[:, 0:n], r[:, 0:n], neg_half[:, 0:n], ALU.pow), v)
            yield None
            for i in range(n):
                o = DVE.do(lambda e, i=i: e.tensor_scalar(dst[i], src[i], m[:, i, 0:1], r[:, i:i + 1],
                                                          ALU.subtract, ALU.mult), w, *dst_free)
            yield o

        last = {}

        def g(name):
            return last.get(name)

        ready3 = {}

        def prepare(b):
            xb, cb = x_buf[b % 3], ctx_buf[b % 2]
            mx_, mc_ = loaded[b]
            for o in norm_rows([xb[:, i, :] for i in range(HALF)], [xn[:, i, :] for i in range(HALF)],
                               stat, mv, rstd, [mx_], [g("xn_read"), g("xn_read2")]):
                xn_ok = o
                yield
            for w, src, dst, col, rdy in ((theta_w, cb, theta, 0, mc_), (phi_w, xn, phi, 1, xn_ok)):
                bk = misc.take()
                for k in range(HALF):
                    m = mm(bk.ap[:, :], w[:, k, :], src[:, k, :], k == 0, k == HALF - 1, rdy, *bk.free)
                s = ACTE.do(lambda e, bk=bk, dst=dst, col=col: e.activation(
                    dst[:, :], bk.ap[:, :], ACT.Identity, bias=lat_b[:, col:col + 1]), m, g("scores_read"))
                bk.free = [s]
                yield
            tp_ok = s
            bk = misc.take()
            for c in range(C):
                for k in range(HALF):
                    m = mm(bk.ap[:, c * P:(c + 1) * P], xn[:, k, c * P:(c + 1) * P], g_w[:, k, :], k == 0,
                           k == HALF - 1, *bk.free)
            xn_read_a = m
            g_ok = ACTE.do(lambda e, bk=bk: e.copy(g_sb[:, :], bk.ap[:, :]), m, g("lat_mm"))
            bk.free = [g_ok]
            yield
            exps = []
            for c in range(C):
                bk = misc.take()
                m = mm(bk.ap[:, :], theta[:, c * P:(c + 1) * P], phi[:, :], True, True, tp_ok, *bk.free)
                last["scores_read"] = m
                r = DVE.do(lambda e, bk=bk, c=c: e.tensor_reduce(nmax1[:, c:c + 1], bk.ap[:, :], X, ALU.max), m, g("exp1"))
                n = DVE.do(lambda e, c=c: e.tensor_scalar(nmax1[:, c:c + 1], nmax1[:, c:c + 1], -1.0, None, ALU.mult), r)
                s = ACTE.do(lambda e, bk=bk, c=c: e.activation(prob[:, c, :], bk.ap[:, :], ACT.Exp,
                                                              bias=nmax1[:, c:c + 1], accum_out=sum1[:, c:c + 1]),
                            n, g("prob_tr"), g("sum_read"))
                bk.free = [s]
                exps.append(s)
                yield
            last["exp1"] = s
            r = DVE.do(lambda e: e.reciprocal(sum1[:, :], sum1[:, :]), s)
            norm = []
            for c in range(C):
                norm.append(DVE.do(lambda e, c=c: e.tensor_scalar(prob[:, c, :], prob[:, c, :], sum1[:, c:c + 1],
                                                                  None, ALU.mult), r))
            last["sum_read"] = norm[-1]
            yield
            for j in range(C):
                bk = misc.take()
                for c in range(C):
                    m = tr(bk.ap[:, c * P:(c + 1) * P], prob[:, c, j * P:(j + 1) * P], ident[:, :], norm[c], *bk.free)
                last["prob_tr"] = m
                s = ACTE.do(lambda e, bk=bk, j=j: e.copy(prob_t[:, j, :], bk.ap[:, :]), m, g("lat_mm"))
                bk.free = [s]
                yield
            bk = misc.take()
            for j in range(C):
                m = mm(bk.ap[:, :], g_sb[:, j * P:(j + 1) * P], prob_t[:, j, :], j == 0, j == C - 1, s, g_ok, *bk.free)
            last["lat_mm"] = m
            s = DVE.do(lambda e, bk=bk: e.tensor_scalar(lat[:, :], bk.ap[:, :], lat_b[:, 2:3], None, ALU.add),
                       m, g("out_mm"))
            bk.free = [s]
            st = DVE.do(lambda e: e.bn_stats(lst[:, :], lat[:, :]), s)
            ag = DVE.do(lambda e: e.bn_aggr(lmv[:, :], lst[:, :]), st)
            cp = DVE.do(lambda e: e.tensor_copy(lmo[:, 0:1], lmv[:, 0:1]), ag)
            sq = DVE.do(lambda e: e.scalar_tensor_tensor(out=lmo[:, 1:2], in0=lmv[:, 0:1], scalar=lmv[:, 0:1],
                                                         in1=lmv[:, 1:2], op0=ALU.mult, op1=ALU.add), ag)
            yield
            yield
            bk = misc.take()
            m = mm(bk.ap[:, 0:2], mean_w[:, :], lmo[:, :], True, True, sq, cp, *bk.free)
            cp = DVE.do(lambda e, bk=bk: e.tensor_copy(ltot[:, 0:2], bk.ap[:, 0:2]), m)
            bk.free = [cp]
            v1 = DVE.do(lambda e: e.scalar_tensor_tensor(out=ltot[:, 2:3], in0=ltot[:, 0:1], scalar=ltot[:, 0:1],
                                                         in1=ltot[:, 1:2], op0=ALU.mult, op1=ALU.subtract), cp)
            v2 = POOL.do(lambda e: e.tensor_scalar(ltot[:, 3:4], ltot[:, 2:3], -1.0, EPS, ALU.mult, ALU.add), v1)
            v3 = POOL.do(lambda e: e.tensor_tensor(ltot[:, 3:4], ltot[:, 3:4], neg_half[:, 0:1], ALU.pow), v2)
            yield
            n1 = DVE.do(lambda e: e.tensor_scalar(lat[:, :], lat[:, :], ltot[:, 0:1], ltot[:, 3:4],
                                                  ALU.subtract, ALU.mult), v3)
            n2 = POOL.do(lambda e: e.tensor_tensor(lat[:, :], lat[:, :], ln_gamma[:, :], ALU.mult), n1)
            n3 = POOL.do(lambda e: e.tensor_tensor(lat[:, :], lat[:, :], ln_beta[:, :], ALU.add), n2)
            n4 = POOL.do(lambda e: e.tensor_scalar(lat[:, :], lat[:, :], 0.0, None, ALU.max), n3)
            yield
            yield
            for k in range(HALF):
                bk = misc.take()
                m = mm(bk.ap[:, :], out_w[:, k * P:(k + 1) * P], lat[:, :], True, True, n4, *bk.free)
                last["out_mm"] = m
                r = DVE.do(lambda e, bk=bk, k=k: e.scalar_tensor_tensor(
                    out=res[:, :], in0=bk.ap[:, :], scalar=out_b[:, k:k + 1], in1=cb[:, k, :],
                    op0=ALU.add, op1=ALU.add), m, g("res_read"), mc_)
                bk.free = [r]
                x1 = POOL.do(lambda e, k=k: e.tensor_tensor(xb[:, k, :], xb[:, k, :], res[:, :], ALU.add), r)
                last["res_read"] = x1
                yield
            for j2 in range(C // 2):
                bk = misc.take()
                for j in range(2):
                    for k in range(HALF):
                        m = tr(bk.ap[:, (j * HALF + k) * P:(j * HALF + k + 1) * P],
                               cb[:, k, (2 * j2 + j) * P:(2 * j2 + j + 1) * P], ident[:, :], mc_, *bk.free)
                for j in range(2):
                    s = ACTE.do(lambda e, bk=bk, j=j, j2=j2: e.copy(
                        v_t[b % 2][:, 2 * j2 + j, :, 0:DQ],
                        bk.ap[:, j * 256:(j + 1) * 256].rearrange("p (h d) -> p h d", d=DQ)), m, g(("pv_mm", b - 2)))
                bk.free = [s]
                yield
            vt_ok = s
            last["ctx_tr"] = m

            def stack_parts(src, src_ok, dst, parts, done, what):
                h_ok = ACTE.do(lambda e: e.copy(hi[:, :, :], src), src_ok, g("stacked"))
                l_ok = POOL.do(lambda e: e.tensor_tensor(lo[:, :, :], src, hi[:, :, :].bitcast(F32), ALU.subtract),
                               h_ok)
                mark = None
                for n, part in enumerate(parts):
                    for hq in range(HPH):
                        mark = SP.dma(lambda e, n=n, hq=hq, part=part: e.dma_start(
                            dst[n * DQ:(n + 1) * DQ, hq:NHEAD:HPH, :].bitcast(F32),
                            part[hq * DQ:(hq + 1) * DQ, :, :].bitcast(F32)),
                            done, h_ok, l_ok, g((what, b - 2)), g(("st_mm", b - 2)))
                last["stacked"] = mark
                return mark, l_ok

            ks_ok, ck = stack_parts(cb[:, :, :], mc_, k_st[b % 2], (hi, hi, lo), k_in[b % 2], "s_mm")
            ctx_free[b % 2] = [ck, last["ctx_tr"], r]
            yield
            for o in norm_rows([xb[:, i, :] for i in range(HALF)], [xn[:, i, :] for i in range(HALF)],
                               stat, mv, rstd, [x1], [xn_read_a]):
                xn_ok = o
                yield
            for k in range(HALF):
                bk = misc.take()
                for c in range(C):
                    m = tr(bk.ap[:, c * P:(c + 1) * P], xn[:, k, c * P:(c + 1) * P], ident[:, :], xn_ok, *bk.free)
                last["xn_read"] = m
                t_ok = ACTE.do(lambda e, bk=bk: e.copy(x_t[:, :, :], bk.ap[:, :].rearrange("p (c q) -> p c q", c=C)),
                               m, g("ffn_mm"))
                bk.free = [t_ok]
                yield
                bk = misc.take()
                for c in range(C):
                    m = mm(bk.ap[:, 0:NE + NR], x_t[:, c, :], lora_in[:, c, :], c == 0, c == C - 1, t_ok, *bk.free)
                r = DVE.do(lambda e, bk=bk: e.tensor_copy(rl[:, :], bk.ap[:, 0:NE + NR]), m)
                bk.free = [r]
                r = DVE.do(lambda e: e.max(top2[:, :], rl[:, 0:NE]), r)
                i1 = DVE.do(lambda e: e.max_index(top2i[:, :], top2[:, :], rl[:, 0:NE]), r)
                d1 = DVE.do(lambda e: e.tensor_tensor(gsc[:, 0:1], top2[:, 1:2], top2[:, 0:1], ALU.subtract), r)
                e1 = ACTE.do(lambda e: e.activation(gsc[:, 1:2], gsc[:, 0:1], ACT.Exp), d1)
                f1 = DVE.do(lambda e: e.tensor_copy(top2f[:, :], top2i[:, 0:2]), i1)
                yield
                a1 = DVE.do(lambda e: e.tensor_scalar(gsc[:, 2:3], gsc[:, 1:2], 1.0, 1.0 / dims["LORA_SCALE"],
                                                      ALU.add, ALU.mult), e1)
                a2 = DVE.do(lambda e: e.reciprocal(gsc[:, 3:4], gsc[:, 2:3]), a1)
                a3 = DVE.do(lambda e: e.tensor_tensor(gsc[:, 4:5], gsc[:, 3:4], gsc[:, 1:2], ALU.mult), a2)
                for n in range(2):
                    a4 = DVE.do(lambda e, n=n: e.tensor_scalar(gate[:, n, :], iota8[:, :], top2f[:, n:n + 1],
                                                               gsc[:, 3 + n:4 + n], ALU.is_equal, ALU.mult), a3, f1)
                a5 = DVE.do(lambda e: e.tensor_tensor(gate[:, 0, :], gate[:, 0, :], gate[:, 1, :], ALU.add), a4)
                a6 = DVE.do(lambda e: e.tensor_tensor(
                    gated[:, 0:NR].rearrange("p (n r) -> p n r", r=NRANK),
                    rl[:, NE:NE + NR].rearrange("p (n r) -> p n r", r=NRANK),
                    gate[:, 0, :].unsqueeze(2).to_broadcast([P, NE, NRANK]), ALU.mult), a5, g("gated_tr"))
                yield
                bk = misc.take()
                m = tr(bk.ap[0:NF, 0:P], gated[:, :], ident[:, :], a6, *bk.free)
                last["gated_tr"] = m
                gt = ACTE.do(lambda e, bk=bk: e.copy(gated_t[:, :], bk.ap[0:NF, 0:P]), m, g("ffn_mm"))
                bk.free = [gt]
                bk = misc.take()
                for c in range(C):
                    m = mm(bk.ap[:, :], x_t[:, c, :], base_w[:, c, :], c == 0, False, *bk.free)
                yield
                m = mm(bk.ap[:, :], gated_t[:, :], lora_out[:, :], False, True, gt)
                last["ffn_mm"] = m
                x2 = DVE.do(lambda e, bk=bk, k=k: e.tensor_tensor(xb[:, k, :], bk.ap[:, :], xb[:, k, :], ALU.add), m)
                bk.free = [x2]
                yield
            for o in norm_rows([xb[:, i, :] for i in range(HALF)], [xn[:, i, :] for i in range(HALF)],
                               stat, mv, rstd, [x2], [last["xn_read"]]):
                xn_ok = o
                yield
            qs_ok, lq = stack_parts(xn[:, :, :], xn_ok, q_st[b % 2], (hi, lo, hi), q_in[b % 2], "s_mm")
            last["xn_read"] = lq
            ready3[b] = (qs_ok, ks_ok, vt_ok, x2)
            yield

        k_in = [arrivals(f"k_in{i}") for i in range(2)]
        q_in = [arrivals(f"q_in{i}") for i in range(2)]

        s_ring, st_ring = Ring(banks[0:2]), Ring(banks[2:4])
        pv_ring = Ring(banks[4:6])
        pt_free = [None] * 4
        attended = {}

        def attend(b, fill):
            qs, ks, vt, xb = q_st[b % 2], k_st[b % 2], v_t[b % 2], x_buf[b % 3]
            qs_ok, ks_ok, vt_ok, x2 = ready3[b]

            def score_chunk(h, c):
                bk = s_ring.take()
                m = mm(bk.ap[:, :], qs[0:SK, h, c * P:(c + 1) * P], ks[0:SK, h, :], True, True, qs_ok, ks_ok, *bk.free)
                last[("s_mm", b)] = m
                r = DVE.do(lambda e: e.tensor_reduce(mx[h % 2][:, c:c + 1], bk.ap[:, :], X, ALU.max), m,
                           g(("mx_read", h % 2)))
                bk.free = [r]
                return r

            def max_cols(h, r):
                mc = max_col[h % 2]
                m1 = DVE.do(lambda e: e.tensor_scalar(mc[:, :, SK].bitcast(F32R), mx[h % 2][:, :], -1.0, None, ALU.mult),
                            r, g(("mc_tr", h % 2)))
                m2 = DVE.do(lambda e: e.scalar_tensor_tensor(out=mc[:, :, SK + 1], in0=mx[h % 2][:, :], scalar=-1.0,
                                                             in1=mc[:, :, SK], op0=ALU.mult, op1=ALU.subtract), m1)
                last[("mx_read", h % 2)] = m2
                return m2

            def max_rows(h, m2):
                mc = max_col[h % 2]
                bk = misc.take()
                for c in range(C):
                    m = tr(bk.ap[0:SKM, c * P:(c + 1) * P], mc[:, c, :], ident[:, :], m2, *bk.free)
                last[("mc_tr", h % 2)] = m
                s = ACTE.do(lambda e, bk=bk: e.copy(qs[SK:SKM, h, :], bk.ap[SK:SKM, :]), m, g(("st_mm", b - 2)))
                bk.free = [s]
                return s

            r = None
            for c in range(C):
                r = score_chunk(0, c)
            rows = max_rows(0, max_cols(0, r))
            pv = None
            for h in range(NHEAD):
                if h % 2 == 0:
                    pv = pv_ring.take()
                pend = None
                base = 2 * DQ * (h % 2)

                def weighted(j, s, slot, h=h, base=base, pv=pv):
                    m = mm(pv.ap[base:base + 2 * DQ, :], vt[:, j, h, :], p_t[slot][:, :], j == 0, j == C - 1, s, vt_ok,
                           *(pv.free if j == 0 and h % 2 == 0 else []))
                    pt_free[slot] = m
                    last[("pv_mm", b)] = m
                    return m

                for j in range(C):
                    bk = st_ring.take()
                    m = mm(bk.ap[:, :], ks[0:SKM, h, j * P:(j + 1) * P], qs[0:SKM, h, :], True, True, rows, *bk.free)
                    last[("st_mm", b)] = m
                    slot = (h * C + j) % 4
                    s = ACTE.do(lambda e, bk=bk, slot=slot: e.activation(p_t[slot][:, :], bk.ap[:, :], ACT.Exp,
                                                                        scale=SCALE), m, pt_free[slot])
                    bk.free = [s]
                    if h + 1 < NHEAD:
                        r = score_chunk(h + 1, j)
                    if pend is not None:
                        weighted(*pend)
                    pend = (j, s, slot)
                    fill()
                if h + 1 < NHEAD:
                    m2 = max_cols(h + 1, r)
                m = weighted(*pend)
                if h + 1 < NHEAD:
                    rows = max_rows(h + 1, m2)
                if h % 2 == 1:
                    n = h // 2 % 2
                    rc = DVE.do(lambda e, pv=pv, n=n: e.reciprocal(rec[n][:, :], pv.ap[:, :]), m, g(("rec_read", n)))
                    half = h // HPH
                    for i in range(2):
                        q = (h - 1 + i) % HPH * DQ
                        o = DVE.do(lambda e, pv=pv, n=n, i=i, q=q, half=half: e.scalar_tensor_tensor(
                            out=att[half][q:q + DQ, :], in0=pv.ap[2 * DQ * i:2 * DQ * i + DQ, :],
                            scalar=gamma1[2 * DQ * i:2 * DQ * i + DQ, 0:1],
                            in1=rec[n][2 * DQ * i + DQ:2 * DQ * (i + 1), :], op0=ALU.mult, op1=ALU.mult),
                            rc, g(("att_read", half)))
                    last[("rec_read", n)] = o
                    pv.free = [o]
                    if h % HPH == HPH - 1:
                        x3 = POOL.do(lambda e, half=half: e.tensor_tensor(xb[:, half, :], xb[:, half, :],
                                                                          att[half][:, :], ALU.add), o, x2)
                        last[("att_read", half)] = x3
                        attended[(b, half)] = x3

        out_in = [arrivals(f"out_in{i}") for i in range(3)]
        sent = [arrivals(f"sent{i}") for i in range(2)]
        sent_mark = [None, None]
        out_marks = [None] * 3

        def dispatch(b):
            xb = x_buf[b % 3]
            x3 = attended[(b, HALF - 1)]
            x3a = attended[(b, 0)]
            dst = out[b * HALF * P:(b + 1) * HALF * P, :].rearrange("(h p) t -> p h t", p=P)
            om = SP.dma(lambda e: e.dma_start(dst, xb[:, :, :]), out_in[b % 3], x3, x3a)
            out_marks[b % 3] = om
            for k in range(HALF):
                tile = b * HALF + k
                rw, si = row[tile % 2], slot_i[tile % 2]
                for o in norm_rows([xb[:, k, :]], [rw[:, 0:T]], stat4, mv4, rstd4, [x3, x3a], [sent_mark[tile % 2]]):
                    xn_ok = o
                    yield
                no = DVE.do(lambda e, rw=rw, tile=tile: e.tensor_scalar(rw[:, T:T + 1].bitcast(I32), row_no[:, 0:1],
                                                                        float(tile * P), None, ALU.add))
                bk = misc.take()
                for c in range(C):
                    m = tr(bk.ap[:, c * P:(c + 1) * P], rw[:, c * P:(c + 1) * P], ident[:, :], xn_ok, *bk.free)
                t_ok = ACTE.do(lambda e, bk=bk: e.copy(x_t2[:, :, :], bk.ap[:, :].rearrange("p (c q) -> p c q", c=C)),
                               m, g("route_mm"))
                bk.free = [t_ok]
                yield
                bk = misc.take()
                for c in range(C):
                    m = mm(bk.ap[:, 0:NEXP], x_t2[:, c, :], route_w[:, c, :], c == 0, c == C - 1, t_ok, *bk.free)
                last["route_mm"] = m
                r = DVE.do(lambda e, bk=bk: e.tensor_reduce(rt[:, 0:1], bk.ap[:, 0:NEXP], X, ALU.max), m)
                r = DVE.do(lambda e: e.tensor_scalar(rt[:, 1:2], rt[:, 0:1], -1.0, None, ALU.mult), r)
                s = ACTE.do(lambda e, bk=bk: e.activation(ex[:, :], bk.ap[:, 0:NEXP], ACT.Exp, bias=rt[:, 1:2],
                                                          accum_out=rt[:, 2:3]), r)
                bk.free = [s]
                yield
                r = DVE.do(lambda e: e.reciprocal(rt[:, 3:4], rt[:, 2:3]), s)
                r = DVE.do(lambda e: e.tensor_scalar(pr[:, :], ex[:, :], rt[:, 3:4], None, ALU.mult), r)
                r = DVE.do(lambda e: e.max(top8[:, :], pr[:, :]), r)
                t8 = DVE.do(lambda e: e.match_replace(out=repl[:, :], in_to_replace=top8[:, :], in_values=pr[:, :],
                                                      imm_value=-1.0), r)
                s8 = DVE.do(lambda e: e.tensor_reduce(rt[:, 4:5], top8[:, :], X, ALU.add), r)
                mk = DVE.do(lambda e: e.tensor_scalar(mask[:, :], repl[:, :], 0.0, None, ALU.is_lt), t8)
                r8 = DVE.do(lambda e: e.reciprocal(rt[:, 5:6], rt[:, 4:5]), s8)
                wt = DVE.do(lambda e, rw=rw: e.tensor_scalar(rw[:, T + 1:ROW], pr[:, :], rt[:, 5:6], None, ALU.mult), r8)
                yield
                bk = misc.take()
                m = mm(bk.ap[:, 0:NEXP], below[:, :], mask[:, :], True, False, mk, *bk.free)
                m = mm(bk.ap[:, 0:NEXP], ones[:, :], seen[:, :], False, True, g("seen"))
                sn = DVE.do(lambda e: e.tensor_tensor(seen[:, :], seen[:, :], mask[:, :], ALU.add), m)
                last["seen"] = sn
                o1 = DVE.do(lambda e, bk=bk: e.tensor_scalar(over[:, :], bk.ap[:, 0:NEXP], float(CAP),
                                                             float(2 * NSLOT), ALU.is_ge, ALU.mult), m)
                o2 = DVE.do(lambda e, bk=bk: e.tensor_tensor(grid[:, :], bk.ap[:, 0:NEXP], expert_off[:, :], ALU.add), m)
                bk.free = [o2]
                o3 = DVE.do(lambda e: e.tensor_tensor(grid[:, :], grid[:, :], over[:, :], ALU.add), o2, o1)
                o4 = DVE.do(lambda e: e.tensor_tensor(grid[:, :], grid[:, :], mask[:, :], ALU.mult), o3)
                o5 = DVE.do(lambda e: e.max(slot8[:, :], grid[:, :]), o4)
                o6 = DVE.do(lambda e, si=si: e.tensor_scalar(si[:, :], slot8[:, :], -1.0, None, ALU.add), o5,
                            sent_mark[tile % 2])
                yield
                for k8 in range(TOPK):
                    mark = POOL.dma(lambda e, k8=k8, rw=rw, si=si: e.indirect_dma_start(
                        out=slots_dram, out_offset=bass.IndirectOffsetOnAxis(ap=si[:, k8:k8 + 1].bitcast(U32), axis=0),
                        in_=rw[:, :], in_offset=None, bounds_check=NSLOT - 1, oob_is_err=False),
                        sent[tile % 2], o6, wt, no, xn_ok, fill_mark)
                    if k8 % 2:
                        yield
                sent_mark[tile % 2] = mark
            x_free[b % 3] = [om, xn_ok]

        def run_all(gen):
            for _ in gen:
                pass

        load_batch(1)
        run_all(prepare(0))
        for b in range(B):
            todo = []
            if b >= 1:
                todo.append(dispatch(b - 1))
            if b + 1 < B:
                todo.append(prepare(b + 1))

            def fill(todo=todo):
                for gen in list(todo):
                    for _ in range(PACE):
                        try:
                            next(gen)
                        except StopIteration:
                            todo.remove(gen)
                            break

            attend(b, fill)
            for gen in todo:
                run_all(gen)
            if b + 2 < B:
                load_batch(b + 2)
        run_all(dispatch(B - 1))

        end_a = [PE.last, ACTE.last, DVE.last]
        sent_all = [m for m in sent_mark if m is not None]
        small.close()
        NB = 3
        W = lambda name, shape, dt=F32: sb(name, shape, dt)
        gu = [W(f"gate_up{i}", [P, C, 2 * INNER]) for i in range(NB)]
        dn = [W(f"down{i}", [IC, 2, T]) for i in range(NB)]
        xe = [W(f"x_slots{i}", [P, 2, ROW]) for i in range(NB)]
        xet = [W(f"x_slots_t{i}", [P, C, P]) for i in range(3)]
        act_g = [W(f"silu{i}", [P, INNER]) for i in range(2)]
        hid = [W(f"hidden{i}", [P, INNER]) for i in range(2)]
        hid_t = [W(f"hidden_t{i}", [IC, 2, P]) for i in range(2)]
        ye = [W(f"y_slots{i}", [P, 2, T]) for i in range(2)]
        e_in = [arrivals(f"expert_in{i}") for i in range(NB)]
        added = [arrivals(f"added{i}") for i in range(2)]
        xt_ring, gu_ring, ht_ring, y_ring = (Ring(banks[2 * i:2 * i + 2]) for i in range(4))
        e_mark, y_mark, added_mark = {}, {}, [None, None]
        xslot_read, gu_read, dn_read = {}, {}, {}
        SP.wait(*end_a, *sent_all, *[m for m in out_marks if m])

        def load_expert(e_):
            i = e_ % NB
            src = slots_dram[e_ * CAP:(e_ + 1) * CAP, :].rearrange("(c p) w -> p c w", p=P)
            SP.dma(lambda e: e.dma_start(gu[i][:, :, :], a["gate_up"][e_]), e_in[i], gu_read.get(e_ - NB))
            SP.dma(lambda e: e.dma_start(dn[i][:, :, :], a["down"][e_]), e_in[i], dn_read.get(e_ - NB))
            e_mark[e_] = SP.dma(lambda e: e.dma_start(xe[i][:, :, :], src), e_in[i], xslot_read.get(e_ - NB),
                                y_mark.get(e_ - NB))

        st = {}

        def turn(u):
            e_, s = divmod(u, 2)
            i = e_ % NB
            bk = xt_ring.take()
            for c in range(C):
                m = tr(bk.ap[:, c * P:(c + 1) * P], xe[i][:, s, c * P:(c + 1) * P], ident[:, :], e_mark[e_], *bk.free)
            o = DVE.do(lambda e: e.tensor_copy(xet[u % 3][:, :, :], bk.ap[:, :].rearrange("p (c q) -> p c q", c=C)), m,
                       st.get(("gu_mm", u - 3)))
            bk.free = [o]
            st[("xt", u)] = o

        def up(u):
            e_, s = divmod(u, 2)
            i = e_ % NB
            bk = gu_ring.take()
            for c in range(C):
                m = mm(bk.ap[:, 0:2 * INNER], xet[u % 3][:, c, :], gu[i][:, c, :], c == 0, c == C - 1, st[("xt", u)],
                       *bk.free)
            st[("gu_mm", u)] = gu_read[e_] = m
            o = ACTE.do(lambda e: e.activation(act_g[u % 2][:, :], bk.ap[:, 0:INNER], ACT.Silu), m,
                        st.get(("hid", u - 2)))
            h = DVE.do(lambda e: e.tensor_tensor(hid[u % 2][:, :], bk.ap[:, INNER:2 * INNER], act_g[u % 2][:, :],
                                                 ALU.mult), o, st.get(("hid_tr", u - 2)))
            bk.free = [h]
            st[("hid", u)] = h

        def turn_hidden(u):
            bk = ht_ring.take()
            for n in range(2):
                m = tr(bk.ap[0:IC, n * P:(n + 1) * P], hid[u % 2][:, n * IC:(n + 1) * IC], ident[:, :], st[("hid", u)],
                       *bk.free)
            st[("hid_tr", u)] = m
            o = ACTE.do(lambda e: e.copy(hid_t[u % 2][:, :, :], bk.ap[0:IC, 0:2 * P].rearrange("p (n q) -> p n q", n=2)),
                        m, st.get(("y_mm", u - 2)))
            bk.free = [o]
            st[("ht", u)] = o

        def down(u):
            e_, s = divmod(u, 2)
            i = e_ % NB
            bk = y_ring.take()
            for n in range(2):
                m = mm(bk.ap[:, :], hid_t[u % 2][:, n, :], dn[i][:, n, :], n == 0, n == 1, st[("ht", u)], *bk.free)
            st[("y_mm", u)] = dn_read[e_] = m
            o = ACTE.do(lambda e: e.activation(ye[e_ % 2][:, s, :], bk.ap[:, :], ACT.Copy,
                                               scale=xe[i][:, s, T + 1 + e_:T + 2 + e_]), m, added_mark[e_ % 2])
            bk.free = [o]
            st[("y", u)] = xslot_read[e_] = o
            if s == 1:
                prev = y_mark.get(e_ - 1)
                for q in range(2):
                    y_mark[e_] = POOL.dma(lambda e, q=q: e.indirect_dma_start(
                        out=out, out_offset=bass.IndirectOffsetOnAxis(ap=xe[i][:, q, T:T + 1].bitcast(U32), axis=0),
                        in_=ye[e_ % 2][:, q, :], in_offset=None, compute_op=ALU.add),
                        added[e_ % 2], o, st[("y", u - 1)], prev, e_mark[e_])
                added_mark[e_ % 2] = y_mark[e_]

        U = 2 * NEXP
        for e_ in range(min(2, NEXP)):
            load_expert(e_)
        for line in (DVE, ACTE, PE, POOL):
            line.wait(*end_a)
        for line in (DVE, ACTE):
            line.wait(*sent_all)
        for t in range(-3, U):
            if t >= 0 and t % 2 == 0 and t // 2 + 2 < NEXP:
                load_expert(t // 2 + 2)
            if 0 <= t + 3 < U:
                turn(t + 3)
            if 0 <= t + 2 < U:
                up(t + 2)
            if 0 <= t + 1 < U:
                turn_hidden(t + 1)
            if t >= 0:
                down(t)
        SP.wait(*[m for m in added_mark if m], *[m for m in out_marks if m], fill_mark, *sent_all)

        lines = (("tensor", PE), ("vector", DVE), ("scalar", ACTE), ("gpsimd", POOL), ("sync", SP))
        for _, line in lines:
            line.number()
        block = stack.enter_context(nc.Block())

        @block.tensor
        def _(e):
            PE.play(e)

        @block.vector
        def _(e):
            DVE.play(e)

        @block.scalar
        def _(e):
            ACTE.play(e)

        @block.gpsimd
        def _(e):
            POOL.play(e)

        @block.sync
        def _(e):
            SP.play(e)


PACE = 2


def kernel(x, ctx_2048, L0_xattn_theta_w, L0_xattn_theta_b, L0_xattn_phi_w, L0_xattn_phi_b, L0_xattn_g_w,
           L0_xattn_g_b, L0_xattn_ln_gamma, L0_xattn_ln_beta, L0_xattn_out_w, L0_xattn_out_b, L0_ffn_W_base,
           L0_ffn_b_base, L0_ffn_W_router, L0_ffn_A_w, L0_ffn_B_w, L1_xattn_gamma, L1_ffn_router_weight,
           L1_ffn_gate_proj, L1_ffn_up_proj, L1_ffn_down_proj):
    import concourse.bacc as _bacc
    from concourse.bass_utils import run_bass_kernel_spmd as _run

    n = np.asarray
    B, rows, T = x.shape
    HALF = rows // P
    NE, NRANK, _ = L0_ffn_A_w.shape
    NEXP, D, INNER = L1_ffn_gate_proj.shape
    dims = dict(B=B, HALF=HALF, T=T, L=L0_xattn_theta_w.shape[0], NHEAD=8, DQ=rows // 8, NE=NE, NRANK=NRANK,
                NEXP=NEXP, CAP=2 * (2 * 512 * 8) // NEXP, TOPK=8, INNER=INNER, LORA_SCALE=16.0 / NRANK)
    CAP = dims["CAP"]
    gate_up = np.concatenate([n(L1_ffn_gate_proj), n(L1_ffn_up_proj)], axis=2)
    gate_up = gate_up.reshape(NEXP, D // P, P, 2 * INNER).transpose(0, 2, 1, 3)
    down = n(L1_ffn_down_proj).reshape(NEXP, 2, INNER // 2, D).transpose(0, 2, 1, 3)
    arrays = {
        "x": n(x), "ctx": n(ctx_2048),
        "theta_wT": n(L0_xattn_theta_w).T, "phi_wT": n(L0_xattn_phi_w).T, "g_wT": n(L0_xattn_g_w).T,
        "lat_b": np.stack([n(L0_xattn_theta_b), n(L0_xattn_phi_b), n(L0_xattn_g_b)], axis=1),
        "ln_gamma": n(L0_xattn_ln_gamma), "ln_beta": n(L0_xattn_ln_beta),
        "out_wT": n(L0_xattn_out_w).T, "out_b": n(L0_xattn_out_b).reshape(HALF, P).T,
        "base_wT": n(L0_ffn_W_base).T,
        "lora_in": np.concatenate([n(L0_ffn_W_router), n(L0_ffn_A_w).reshape(NE * NRANK, T)], axis=0).T,
        "lora_out": np.concatenate([n(L0_ffn_B_w).transpose(0, 2, 1).reshape(NE * NRANK, T),
                                    n(L0_ffn_b_base).reshape(1, T)], axis=0),
        "route_w": n(L1_ffn_router_weight),
        "gamma1": np.broadcast_to(n(L1_xattn_gamma).reshape(1, 1), (P, 1)),
        "gate_up": gate_up, "down": down,
    }
    arrays = {f"in_{k}": np.ascontiguousarray(v) for k, v in arrays.items()}
    nc = _bacc.Bacc("TRN2", target_bir_lowering=False, num_devices=1)
    aps = {k[3:]: nc.dram_tensor(k, v.shape, mybir.dt.from_np(v.dtype), kind="ExternalInput").ap()
           for k, v in arrays.items()}
    out = nc.dram_tensor("out_rows", (B * rows + CAP, T), F32, kind="ExternalOutput").ap()
    slots = nc.dram_tensor("slot_rows", (NEXP * CAP, T + 1 + NEXP), F32, kind="Internal").ap()
    build(nc, aps, out, slots, dims)
    r = _run(nc, [arrays], core_ids=[0])
    return r.results[0]["out_rows"][:B * rows].reshape(B, rows, T)
```

```python
from contextlib import ExitStack

import numpy as np

import concourse.bass as bass
from concourse import mybir

ALU = mybir.AluOpType
ACT = mybir.ActivationFunctionType
X = mybir.AxisListType.X
F32 = mybir.dt.float32
F32R = mybir.dt.float32r
I32 = mybir.dt.int32
U32 = mybir.dt.uint32

P = 128
EPS = 1e-5


class Step:

    def __init__(self, line, run):
        self.line, self.run, self.waited, self.count = line, run, False, None


class Line:

    def __init__(self, sem):
        self.sem, self.items = sem, []

    def wait(self, *steps):
        for s in steps:
            if s is not None:
                s.waited = True
                self.items.append(("wait", s))

    def do(self, run, *after):
        self.wait(*after)
        self.last = Step(self, run)
        self.items.append(("do", self.last))
        return self.last

    def dma(self, run, done, *after):
        self.wait(*after)
        mark = done.next()
        self.items.append(("dma", (run, done.sem)))
        return mark

    def number(self):
        n = 0
        for kind, s in self.items:
            if kind == "do" and s.waited:
                n += 1
                s.count = n

    def play(self, engine):
        reached = {}
        for kind, s in self.items:
            if kind == "wait":
                sem, count = (s.line.sem, s.count) if isinstance(s, Step) else (s.sem, s.count)
                if reached.get(id(sem), 0) < count:
                    engine.wait_ge(sem, count)
                    reached[id(sem)] = count
            elif kind == "do":
                ins = s.run(engine)
                if s.waited:
                    ins.then_inc(self.sem, 1)
            else:
                s[0](engine).then_inc(s[1], 16)


class Mark:
    def __init__(self, sem, count):
        self.sem, self.count, self.waited = sem, count, True


class Arrivals:

    def __init__(self, sem):
        self.sem, self.count = sem, 0

    def next(self):
        self.count += 16
        return Mark(self.sem, self.count)


class Bank:

    def __init__(self, ap):
        self.ap, self.free = ap, []


class Ring:
    def __init__(self, banks):
        self.banks, self.n = banks, 0

    def take(self):
        self.n += 1
        return self.banks[(self.n - 1) % len(self.banks)]


def build(nc, a, out, slots_dram, dims):
    B, HALF, T, L, NHEAD, DQ, NE, NEXP, CAP, TOPK, NRANK = (
        dims[k] for k in ("B", "HALF", "T", "L", "NHEAD", "DQ", "NE", "NEXP", "CAP", "TOPK", "NRANK"))
    C = T // P
    NR = NE * NRANK
    NF = NR + 1
    ROWS = B * HALF * P
    INNER = dims["INNER"]
    IC = INNER // 2
    ROW = T + 1 + NEXP
    NSLOT = NEXP * CAP
    SCALE = float(DQ) ** -0.5
    SK = 3 * DQ
    SKM = SK + 2
    HPH = NHEAD // HALF

    stack = ExitStack()
    with stack:
        def sem(name):
            return stack.enter_context(nc.semaphore(name))

        def sb(name, shape, dt=F32, on=stack):
            return on.enter_context(nc.sbuf_tensor(name, shape, dt))

        PE, DVE, ACTE, POOL, SP = (Line(sem(n)) for n in ("pe_done", "dve_done", "act_done", "pool_done", "sp_done"))

        def arrivals(name):
            return Arrivals(sem(name))

        psum = [stack.enter_context(nc.psum_tensor(f"bank{i}", [P, 512], F32)) for i in range(8)]
        banks = [Bank(t) for t in psum]

        def mm(bank_ap, lhsT, rhs, start, stop, *after):
            return PE.do(lambda e: e.matmul(bank_ap, lhsT, rhs, start=start, stop=stop), *after)

        def tr(bank_ap, src, ident_ap, *after):
            return PE.do(lambda e: e.transpose(bank_ap, src, ident_ap), *after)

        small = ExitStack()
        stack.enter_context(small)
        ident = sb("ident", [P, P])
        ones = sb("ones", [P, P])

        def A(name, shape, dt=F32):
            return sb(name, shape, dt, small)

        below = A("below", [P, P])
        mean_w = A("mean_w", [P, P])
        neg_half = A("neg_half", [P, 2])
        iota8 = A("iota8", [P, NE])
        expert_off = A("expert_off", [P, NEXP])
        row_no = A("row_no", [P, 2])
        theta_w = A("theta_w", [P, HALF, L])
        phi_w = A("phi_w", [P, HALF, L])
        g_w = A("g_w", [P, HALF, L])
        lat_b = A("lat_b", [P, 3])
        ln_gamma = A("ln_gamma", [P, T])
        ln_beta = A("ln_beta", [P, T])
        out_w = A("out_w", [P, HALF * P])
        out_b = A("out_b", [P, HALF])
        base_w = A("base_w", [P, C, T])
        lora_in = A("lora_in", [P, C, NE + NR])
        lora_out = A("lora_out", [NF, T])
        route_w = A("route_w", [P, C, NEXP])
        gamma1 = A("gamma1", [P, 1])
        rows = [A(f"row{i}", [P, HALF, ROW]) for i in range(2)]
        fill_row = rows[0]

        weights_in = arrivals("weights_in")

        def load(dst, src):
            return SP.dma(lambda e: e.dma_start(dst, src), weights_in)

        NX = 4
        x_buf = [A(f"x{i}", [P, HALF, T]) for i in range(NX)]
        ctx_buf = [A(f"ctx{i}", [P, HALF, T]) for i in range(2)]
        x_in = [arrivals(f"x_in{i}") for i in range(NX)]
        ctx_in = [arrivals(f"ctx_in{i}") for i in range(2)]
        x_free, ctx_free = [[] for _ in range(NX)], [[], []]
        loaded = {}

        def load_batch(b):
            xb, cb = x_buf[b % NX], ctx_buf[b % 2]
            mx = SP.dma(lambda e: e.dma_start(xb[:, :, :], a["x"][b].rearrange("(h p) t -> p h t", p=P)),
                        x_in[b % NX], *x_free[b % NX])
            mc = SP.dma(lambda e: e.dma_start(cb[:, :, :], a["ctx"][b].rearrange("(h p) t -> p h t", p=P)),
                        ctx_in[b % 2], *ctx_free[b % 2])
            loaded[b] = (mx, mc)

        load_batch(0)
        for h in range(HALF):
            load(theta_w[:, h, :], a["theta_wT"][h * P:(h + 1) * P, :])
            load(phi_w[:, h, :], a["phi_wT"][h * P:(h + 1) * P, :])
            load(g_w[:, h, :], a["g_wT"][h * P:(h + 1) * P, :])
        load(lat_b[:, :], a["lat_b"])
        load(ln_gamma[:, :], a["ln_gamma"])
        load(ln_beta[:, :], a["ln_beta"])
        load(out_w[:, :], a["out_wT"])
        load(out_b[:, :], a["out_b"])
        load(base_w[:, :, :], a["base_wT"].rearrange("(c p) o -> p c o", p=P))
        load(lora_in[:, :, :], a["lora_in"].rearrange("(c p) o -> p c o", p=P))
        load(lora_out[:, :], a["lora_out"])
        load(route_w[:, :, :], a["route_w"].rearrange("(c p) o -> p c o", p=P))
        weights_ready = load(gamma1[:, :], a["gamma1"])

        q_st = [A(f"q_stack{i}", [SKM, NHEAD, T], F32R) for i in range(2)]
        k_st = [A(f"k_stack{i}", [SKM, NHEAD, T], F32R) for i in range(2)]
        v_t = [A(f"v_t{i}", [P, C, NHEAD, 2 * DQ]) for i in range(2)]
        max_col = [A(f"max_col{i}", [P, C, SKM]) for i in range(2)]

        m0 = POOL.do(lambda e: e.memset(ident[:, :], 0.0))
        ident_ok = POOL.do(lambda e: e.affine_select(out=ident[:, :], in_=ident[:, :], compare_op=ALU.not_equal,
                                                     fill=1.0, base=0, pattern=[[-1, P]], channel_multiplier=1), m0)
        ones_ok = POOL.do(lambda e: e.memset(ones[:, :], 1.0))
        mw_ok = POOL.do(lambda e: e.memset(mean_w[:, :], 1.0 / P))
        below_ok = POOL.do(lambda e: e.affine_select(out=below[:, :], in_=ones[:, :], compare_op=ALU.is_gt, fill=0.0,
                                                     base=0, pattern=[[1, P]], channel_multiplier=-1), ones_ok)
        POOL.do(lambda e: e.memset(neg_half[:, :], -0.5))
        POOL.do(lambda e: e.iota(iota8[:, :], pattern=[[1, NE]], base=0, channel_multiplier=0,
                                 allow_small_or_imprecise_dtypes=True))
        POOL.do(lambda e: e.iota(expert_off[:, :], pattern=[[CAP, NEXP]], base=1, channel_multiplier=0,
                                 allow_small_or_imprecise_dtypes=True))
        f0 = POOL.do(lambda e: e.memset(fill_row[:, :, :], 0.0))
        for c in range(2):
            dst = fill_row[:, c, T:T + 1].bitcast(I32)
            fill_ok = POOL.do(lambda e, d=dst, c=c: e.iota(d, pattern=[[0, 1]], base=ROWS + c * P,
                                                           channel_multiplier=1), f0)
        rn = POOL.do(lambda e: e.iota(row_no[:, :], pattern=[[P, 2]], base=0, channel_multiplier=1,
                                      allow_small_or_imprecise_dtypes=True))
        for i in range(2):
            POOL.do(lambda e, t=max_col[i]: e.memset(t[:, :, :], 0.0))
            consts_ok2 = POOL.do(lambda e, t=v_t[i]: e.memset(t[:, :, :, :], 1.0))
            consts_ok = DVE.do(lambda e, t=k_st[i]: e.memset(t[SK:SKM, :, :].bitcast(F32), 1.0))

        slots_filled = arrivals("slots_filled")
        EG = NEXP // 4
        for g in range(4):
            dst = slots_dram[g * EG * CAP:(g + 1) * EG * CAP, :].rearrange("(e c p) w -> p e c w", c=2, p=P)
            for e_ in range(EG):
                d = slots_dram[(g * EG + e_) * CAP:(g * EG + e_ + 1) * CAP, :].rearrange("(c p) w -> p c w", p=P)
                fm = SP.dma(lambda e, d=d: e.dma_start(d, fill_row[:, :, :]), slots_filled, fill_ok, f0)
        spare = out[ROWS:ROWS + CAP, :].rearrange("(c p) t -> p c t", p=P)
        fill_mark = SP.dma(lambda e: e.dma_start(spare, fill_row[:, :, 0:T]), slots_filled)

        xn = A("xn", [P, HALF, T])
        theta = A("theta", [P, T])
        phi = A("phi", [P, T])
        g_sb = A("g_sb", [P, T])
        prob = A("prob", [P, C, T])
        prob_t = A("prob_t", [P, C, T])
        lat = A("lat", [P, T])
        x_t = A("x_t", [P, HALF, C, P])
        x_t4 = A("x_t4", [P, HALF, C, P])
        hi = A("hi", [P, HALF, T], F32R)
        lo = A("lo", [P, HALF, T], F32R)
        row_stat = A("row_stat", [P, HALF, 6])
        row_mv = A("row_mv", [P, HALF, 2])
        row_rstd = A("row_rstd", [P, HALF])
        row_stat4 = A("row_stat4", [P, HALF, 6])
        row_mv4 = A("row_mv4", [P, HALF, 2])
        row_rstd4 = A("row_rstd4", [P, HALF])
        lat_stat = A("lat_stat", [P, 6])
        lat_mv = A("lat_mv", [P, 2])
        lat_mom = A("lat_mom", [P, 2])
        lat_all = A("lat_all", [P, 4])
        neg_max = A("neg_max", [P, C])
        exp_sum = A("exp_sum", [P, C])
        lora_mid = A("lora_mid", [P, HALF, NE + NR])
        top2 = A("top2", [P, HALF, 8])
        top2_at = A("top2_at", [P, HALF, 8], U32)
        top2_f = A("top2_f", [P, HALF, 2])
        gate_s = A("gate_s", [P, 4, HALF])
        gate_2 = A("gate_2", [P, HALF, 2])
        gate = A("gate", [P, HALF, 2, NE])
        gated = A("gated", [P, HALF, NF])
        gated_t = A("gated_t", [NF, HALF, P])
        p_t = [A(f"p_t{i}", [P, T]) for i in range(4)]
        q_max = [A(f"q_max{i}", [P, C]) for i in range(2)]
        pair_sb = [A(f"pair_sb{i}", [P, T]) for i in range(2)]
        sum_inv = A("sum_inv", [P, C, 2])
        att_q = [A(f"att_q{i}", [P, C, 2, 2 * DQ]) for i in range(2)]
        r_max = A("r_max", [P, HALF])
        r_sum = A("r_sum", [P, HALF])
        r_inv = A("r_inv", [P, HALF])
        r_top = A("r_top", [P, HALF])
        r_topi = A("r_topi", [P, HALF])
        r_exp = A("r_exp", [P, HALF, NEXP])
        top8 = A("top8", [P, HALF, TOPK])
        repl = A("repl", [P, HALF, NEXP])
        mask = A("mask", [P, HALF, NEXP])
        seen = A("seen", [P, NEXP])
        over = A("over", [P, HALF, NEXP])
        grid = A("grid", [P, HALF, NEXP])
        slot8 = A("slot8", [P, HALF, TOPK])
        slot_i = [A(f"slot_i{i}", [P, HALF, TOPK], I32) for i in range(2)]

        gated_one = DVE.do(lambda e: e.memset(gated[:, :, :], 1.0))
        seen_ok = DVE.do(lambda e: e.memset(seen[:, :], 0.0))
        for line in (PE, ACTE, DVE, POOL):
            line.wait(weights_ready, consts_ok, consts_ok2, ident_ok, below_ok, mw_ok, rn, gated_one, seen_ok)

        s_ring, st_ring, pv_ring = Ring(banks[0:2]), Ring(banks[2:4]), Ring(banks[4:5])
        prep_ring, side_ring = Ring(banks[5:7]), Ring(banks[7:8])
        last = {}
        g = last.get

        def norm_stats(src, st, m, r, ready):
            for i in range(HALF):
                s = DVE.do(lambda e, i=i: e.bn_stats(st[:, i, :], src[i]), *ready)
                agg = DVE.do(lambda e, i=i: e.bn_aggr(m[:, i, :], st[:, i, :]), s)
            v = POOL.do(lambda e: e.tensor_scalar(r[:, :], m[:, :, 1], EPS, None, ALU.add), agg)
            return POOL.do(lambda e: e.tensor_tensor(r[:, :], r[:, :], neg_half[:, :], ALU.pow), v)

        def norm_apply(src, dst, m, r, *after):
            for i in range(HALF):
                o = DVE.do(lambda e, i=i: e.tensor_scalar(dst[i], src[i], m[:, i, 0:1], r[:, i:i + 1],
                                                          ALU.subtract, ALU.mult), *after)
            return o

        def halves(t):
            return [t[:, i, 0:T] for i in range(HALF)]

        heads_done = []
        ready3 = {}
        k_in = [arrivals(f"k_in{i}") for i in range(2)]
        q_in = [arrivals(f"q_in{i}") for i in range(2)]

        def prepare(b):
            xb, cb = x_buf[b % NX], ctx_buf[b % 2]
            x_ok, c_ok = loaded[b]
            def split_hi(src, src_ok):
                return ACTE.do(lambda e: e.copy(hi[:, :, :], src), src_ok, g("stacked"))

            def stack_rows(dst, part, places, done, *after):
                for n in places:
                    for hq in range(HPH):
                        last["stacked"] = SP.dma(lambda e, n=n, hq=hq: e.dma_start(
                            dst[n * DQ:(n + 1) * DQ, hq:NHEAD:HPH, :].bitcast(F32),
                            part[hq * DQ:(hq + 1) * DQ, :, :].bitcast(F32)),
                            done, g(("s_mm", b - 2)), g(("st_mm", b - 2)), *after)
                return last["stacked"]

            def split_lo(src, h_ok):
                return DVE.do(lambda e: e.tensor_tensor(lo[:, :, :], src, hi[:, :, :].bitcast(F32), ALU.subtract),
                              h_ok, stacked)

            w = norm_stats(halves(xb), row_stat, row_mv, row_rstd, [x_ok])
            yield
            yield
            xn_ok = norm_apply(halves(xb), halves(xn), row_mv, row_rstd, w, g("xn_read"))
            yield
            def project(wt, src, dst, col, rdy):
                bk = prep_ring.take()
                for k in range(HALF):
                    m = mm(bk.ap[:, :], wt[:, k, :], src[:, k, :], k == 0, k == HALF - 1, rdy, *bk.free)
                s = ACTE.do(lambda e: e.activation(dst[:, :], bk.ap[:, :], ACT.Identity, bias=lat_b[:, col:col + 1]),
                            m, g("scores_mm"))
                bk.free = [s]
                return s
            th_ok = project(theta_w, cb, theta, 0, c_ok)
            yield
            phi_ok = project(phi_w, xn, phi, 1, xn_ok)
            yield
            bk = prep_ring.take()
            for c in range(C):
                for k in range(HALF):
                    m = mm(bk.ap[:, c * P:(c + 1) * P], xn[:, k, c * P:(c + 1) * P], g_w[:, k, :], k == 0,
                           k == HALF - 1, *bk.free)
            xn_read = m
            g_ok = ACTE.do(lambda e, bk=bk: e.copy(g_sb[:, :], bk.ap[:, :]), m, g("lat_mm"))
            bk.free = [g_ok]
            yield
            for c in range(C):
                bk = prep_ring.take()
                m = mm(bk.ap[:, :], theta[:, c * P:(c + 1) * P], phi[:, :], True, True, th_ok, phi_ok, *bk.free)
                r = DVE.do(lambda e, bk=bk, c=c: e.tensor_reduce(neg_max[:, c:c + 1], bk.ap[:, :], X, ALU.max), m,
                           g("latent_exp"))
                r = DVE.do(lambda e, c=c: e.tensor_scalar(neg_max[:, c:c + 1], neg_max[:, c:c + 1], -1.0, None,
                                                          ALU.mult), r)
                s = ACTE.do(lambda e, bk=bk, c=c: e.activation(prob[:, c, :], bk.ap[:, :], ACT.Exp,
                                                              bias=neg_max[:, c:c + 1], accum_out=exp_sum[:, c:c + 1]),
                            r, g("prob_tr"), g("exp_sum_read"))
                bk.free = [s]
                if c % 2 or c == 0:
                    yield
            last["scores_mm"], last["latent_exp"] = m, s
            r = DVE.do(lambda e: e.reciprocal(exp_sum[:, :], exp_sum[:, :]), s)
            norm = [DVE.do(lambda e, c=c: e.tensor_scalar(prob[:, c, :], prob[:, c, :], exp_sum[:, c:c + 1],
                                                          None, ALU.mult), r) for c in range(C)]
            last["exp_sum_read"] = norm[-1]
            yield
            for j in range(C):
                bk = prep_ring.take()
                for c in range(C):
                    m = tr(bk.ap[:, c * P:(c + 1) * P], prob[:, c, j * P:(j + 1) * P], ident[:, :], norm[c], *bk.free)
                s = ACTE.do(lambda e, bk=bk, j=j: e.copy(prob_t[:, j, :], bk.ap[:, :]), m, g("lat_mm"))
                bk.free = [s]
                if j % 2:
                    yield
            last["prob_tr"] = m
            bk = prep_ring.take()
            for j in range(C):
                m = mm(bk.ap[:, :], g_sb[:, j * P:(j + 1) * P], prob_t[:, j, :], j == 0, j == C - 1, s, g_ok, *bk.free)
            last["lat_mm"] = m
            s = DVE.do(lambda e, bk=bk: e.tensor_scalar(lat[:, :], bk.ap[:, :], lat_b[:, 2:3], None, ALU.add),
                       m, g("out_mm"))
            bk.free = [s]
            s = DVE.do(lambda e: e.bn_stats(lat_stat[:, :], lat[:, :]), s)
            s = DVE.do(lambda e: e.bn_aggr(lat_mv[:, :], lat_stat[:, :]), s)
            cp = DVE.do(lambda e: e.tensor_copy(lat_mom[:, 0:1], lat_mv[:, 0:1]), s)
            sq = DVE.do(lambda e: e.scalar_tensor_tensor(out=lat_mom[:, 1:2], in0=lat_mv[:, 0:1],
                                                         scalar=lat_mv[:, 0:1], in1=lat_mv[:, 1:2],
                                                         op0=ALU.mult, op1=ALU.add), s)
            yield
            while len(heads_done) < (b - 1) * NHEAD:
                yield
            for j2 in range(C // 2):
                bk = prep_ring.take()
                for j in range(2):
                    for k in range(HALF):
                        m = tr(bk.ap[:, (j * HALF + k) * P:(j * HALF + k + 1) * P],
                               cb[:, k, (2 * j2 + j) * P:(2 * j2 + j + 1) * P], ident[:, :], c_ok, *bk.free)
                for j in range(2):
                    s = ACTE.do(lambda e, bk=bk, j=j, j2=j2: e.activation(
                        v_t[b % 2][:, 2 * j2 + j, :, 0:DQ],
                        bk.ap[:, j * HALF * P:(j + 1) * HALF * P].rearrange("p (h d) -> p h d", d=DQ),
                        ACT.Copy, scale=gamma1[:, 0:1]), m, g(("pv_mm", b - 2)))
                bk.free = [s]
            vt_ok, ctx_tr = s, m
            stacked = g("stacked")
            h_ok = split_hi(cb[:, :, :], c_ok)
            stack_rows(k_st[b % 2], hi, (0, 1), k_in[b % 2], h_ok)
            yield
            k_read = split_lo(cb[:, :, :], h_ok)
            ks_ok = stack_rows(k_st[b % 2], lo, (2,), k_in[b % 2], k_read)
            yield
            bk = prep_ring.take()
            m = mm(bk.ap[:, 0:2], mean_w[:, :], lat_mom[:, :], True, True, sq, cp, *bk.free)
            cp = DVE.do(lambda e, bk=bk: e.tensor_copy(lat_all[:, 0:2], bk.ap[:, 0:2]), m)
            bk.free = [cp]
            v = DVE.do(lambda e: e.scalar_tensor_tensor(out=lat_all[:, 2:3], in0=lat_all[:, 0:1],
                                                        scalar=lat_all[:, 0:1], in1=lat_all[:, 1:2],
                                                        op0=ALU.mult, op1=ALU.subtract), cp)
            v = POOL.do(lambda e: e.tensor_scalar(lat_all[:, 3:4], lat_all[:, 2:3], -1.0, EPS, ALU.mult, ALU.add), v)
            v = POOL.do(lambda e: e.tensor_tensor(lat_all[:, 3:4], lat_all[:, 3:4], neg_half[:, 0:1], ALU.pow), v)
            yield
            n = DVE.do(lambda e: e.scalar_tensor_tensor(out=lat[:, :], in0=lat[:, :], scalar=lat_all[:, 0:1],
                                                        in1=ln_gamma[:, :], op0=ALU.subtract, op1=ALU.mult), v)
            n = DVE.do(lambda e: e.scalar_tensor_tensor(out=lat[:, :], in0=lat[:, :], scalar=lat_all[:, 3:4],
                                                        in1=ln_beta[:, :], op0=ALU.mult, op1=ALU.add), n)
            n = ACTE.do(lambda e: e.activation(lat[:, :], lat[:, :], ACT.Relu), n)
            yield
            for k in range(HALF):
                bk = prep_ring.take()
                m = mm(bk.ap[:, :], out_w[:, k * P:(k + 1) * P], lat[:, :], True, True, n, *bk.free)
                r = DVE.do(lambda e, bk=bk, k=k: e.scalar_tensor_tensor(
                    out=xn[:, k, :], in0=bk.ap[:, :], scalar=out_b[:, k:k + 1], in1=cb[:, k, :],
                    op0=ALU.add, op1=ALU.add), m, xn_read, c_ok)
                bk.free = [r]
                x1 = POOL.do(lambda e, k=k: e.tensor_tensor(xb[:, k, :], xb[:, k, :], xn[:, k, :], ALU.add), r)
            last["out_mm"], res_ok = m, r
            ctx_free[b % 2] = [k_read, ctx_tr, res_ok]
            yield
            yield
            w = norm_stats(halves(xb), row_stat, row_mv, row_rstd, [x1])
            yield
            yield
            xn_ok = norm_apply(halves(xb), halves(xn), row_mv, row_rstd, w, xn_read)
            yield
            for k in range(HALF):
                bk = prep_ring.take()
                for c in range(C):
                    m = tr(bk.ap[:, c * P:(c + 1) * P], xn[:, k, c * P:(c + 1) * P], ident[:, :], xn_ok, *bk.free)
                t_ok = ACTE.do(lambda e, bk=bk, k=k: e.copy(x_t[:, k, :, :],
                                                           bk.ap[:, :].rearrange("p (c q) -> p c q", c=C)),
                               m, g("ffn_mm"))
                bk.free = [t_ok]
            xn_read = m
            yield
            bk = prep_ring.take()
            W1 = NE + NR
            for k in range(HALF):
                for c in range(C):
                    m = mm(bk.ap[:, k * W1:(k + 1) * W1], x_t[:, k, c, :], lora_in[:, c, :], c == 0, c == C - 1,
                           t_ok, *bk.free)
            r = DVE.do(lambda e, bk=bk: e.tensor_copy(
                lora_mid[:, :, :], bk.ap[:, 0:HALF * W1].rearrange("p (k w) -> p k w", k=HALF)), m)
            bk.free = [r]
            for k in range(HALF):
                t2 = DVE.do(lambda e, k=k: e.max(top2[:, k, :], lora_mid[:, k, 0:NE]), r)
                i2 = DVE.do(lambda e, k=k: e.max_index(top2_at[:, k, :], top2[:, k, :], lora_mid[:, k, 0:NE]), t2)
            d = DVE.do(lambda e: e.tensor_tensor(gate_s[:, 0, :], top2[:, :, 1], top2[:, :, 0], ALU.subtract), t2)
            e1 = ACTE.do(lambda e: e.activation(gate_s[:, 1, :], gate_s[:, 0, :], ACT.Exp), d)
            f = DVE.do(lambda e: e.tensor_copy(top2_f[:, :, :], top2_at[:, :, 0:2]), i2)
            yield
            r = DVE.do(lambda e: e.tensor_scalar(gate_s[:, 2, :], gate_s[:, 1, :], 1.0, 1.0 / dims["LORA_SCALE"],
                                                 ALU.add, ALU.mult), e1)
            r = DVE.do(lambda e: e.reciprocal(gate_2[:, :, 0], gate_s[:, 2, :]), r)
            r = DVE.do(lambda e: e.tensor_tensor(gate_2[:, :, 1], gate_2[:, :, 0], gate_s[:, 1, :], ALU.mult), r)
            for k in range(HALF):
                for n in range(2):
                    q = DVE.do(lambda e, k=k, n=n: e.tensor_scalar(gate[:, k, n, :], iota8[:, :],
                                                                   top2_f[:, k, n:n + 1], gate_2[:, k, n:n + 1],
                                                                   ALU.is_equal, ALU.mult), r, f)
            q = DVE.do(lambda e: e.tensor_tensor(gate[:, :, 0, :], gate[:, :, 0, :], gate[:, :, 1, :], ALU.add), q)
            for k in range(HALF):
                q2 = DVE.do(lambda e, k=k: e.tensor_tensor(
                    gated[:, k, 0:NR].rearrange("p (n r) -> p n r", r=NRANK),
                    lora_mid[:, k, NE:NE + NR].rearrange("p (n r) -> p n r", r=NRANK),
                    gate[:, k, 0, :].unsqueeze(2).to_broadcast([P, NE, NRANK]), ALU.mult), q, g("gated_tr"))
            yield
            yield
            bk = prep_ring.take()
            for k in range(HALF):
                m = tr(bk.ap[0:NF, k * P:(k + 1) * P], gated[:, k, :], ident[:, :], q2, *bk.free)
            last["gated_tr"] = m
            gt = ACTE.do(lambda e, bk=bk: e.copy(gated_t[:, :, :],
                                                 bk.ap[0:NF, 0:HALF * P].rearrange("p (k q) -> p k q", k=HALF)),
                         m, g("ffn_mm"))
            bk.free = [gt]
            yield
            for k in range(HALF):
                bk = prep_ring.take()
                for c in range(C):
                    m = mm(bk.ap[:, :], x_t[:, k, c, :], base_w[:, c, :], c == 0, False, *bk.free)
                    if c == 1:
                        yield
                m = mm(bk.ap[:, :], gated_t[:, k, :], lora_out[:, :], False, True, gt)
                x2 = DVE.do(lambda e, bk=bk, k=k: e.tensor_tensor(xb[:, k, :], bk.ap[:, :], xb[:, k, :], ALU.add), m)
                bk.free = [x2]
                yield
            last["ffn_mm"] = m
            w = norm_stats(halves(xb), row_stat, row_mv, row_rstd, [x2])
            yield
            yield
            xn_ok = norm_apply(halves(xb), halves(xn), row_mv, row_rstd, w, xn_read)
            yield
            stacked = g("stacked")
            h_ok = split_hi(xn[:, :, :], xn_ok)
            stack_rows(q_st[b % 2], hi, (0, 2), q_in[b % 2], h_ok)
            yield
            last["xn_read"] = q_read = split_lo(xn[:, :, :], h_ok)
            qs_ok = stack_rows(q_st[b % 2], lo, (1,), q_in[b % 2], q_read)
            ready3[b] = (qs_ok, ks_ok, vt_ok, x2)
            yield

        pt_free = [None] * 4
        attended, rows_ok, col_ok = {}, {}, {}
        tails = []

        def score_chunk(H, c):
            b, h = divmod(H, NHEAD)
            qs_ok, ks_ok, _, _ = ready3[b]
            bk = s_ring.take()
            m = mm(bk.ap[:, :], q_st[b % 2][0:SK, h, c * P:(c + 1) * P], k_st[b % 2][0:SK, h, :], True, True,
                   qs_ok, ks_ok, *bk.free)
            last[("s_mm", b)] = m
            r = DVE.do(lambda e: e.tensor_reduce(q_max[H % 2][:, c:c + 1], bk.ap[:, :], X, ALU.max), m)
            bk.free = [r]
            if c == C - 1:
                mc = max_col[H % 2]
                m1 = DVE.do(lambda e: e.tensor_scalar(mc[:, :, SK].bitcast(F32R), q_max[H % 2][:, :], -1.0, None,
                                                      ALU.mult), r, g(("mc_tr", H % 2)))
                col_ok[H] = DVE.do(lambda e: e.scalar_tensor_tensor(out=mc[:, :, SK + 1], in0=q_max[H % 2][:, :],
                                                                    scalar=-1.0, in1=mc[:, :, SK], op0=ALU.mult,
                                                                    op1=ALU.subtract), m1)

        def max_rows(H):
            b, h = divmod(H, NHEAD)
            mc = max_col[H % 2]
            bk = side_ring.take()
            for c in range(C):
                m = tr(bk.ap[0:SKM, c * P:(c + 1) * P], mc[:, c, :], ident[:, :], col_ok[H], *bk.free)
            last[("mc_tr", H % 2)] = m
            s = ACTE.do(lambda e: e.copy(q_st[b % 2][SK:SKM, h, :], bk.ap[SK:SKM, :]), m, g(("st_mm", b - 2)))
            bk.free = [s]
            rows_ok[H] = s

        pv_bank = {}

        def key_chunk(H, j):
            b, h = divmod(H, NHEAD)
            bk = st_ring.take()
            m = mm(bk.ap[:, :], k_st[b % 2][0:SKM, h, j * P:(j + 1) * P], q_st[b % 2][0:SKM, h, :], True, True,
                   rows_ok[H], *bk.free)
            last[("st_mm", b)] = m
            slot = (H * C + j) % 4
            s = ACTE.do(lambda e: e.activation(p_t[slot][:, :], bk.ap[:, :], ACT.Exp, scale=SCALE), m, pt_free[slot])
            bk.free = [s]
            return H, j, slot, s

        def weighted(H, j, slot, s):
            b, h = divmod(H, NHEAD)
            if j == 0 and h % 2 == 0:
                pv_bank[H // 2] = pv_ring.take()
            pv = pv_bank[H // 2]
            base = 2 * DQ * (h % 2)
            m = mm(pv.ap[base:base + 2 * DQ, :], v_t[b % 2][:, j, h, :], p_t[slot][:, :], j == 0, j == C - 1, s,
                   ready3[b][2], *(pv.free if j == 0 and h % 2 == 0 else []))
            pt_free[slot] = m
            last[("pv_mm", b)] = m
            if j == C - 1:
                heads_done.append(H)
            if j == C - 1 and h % 2 == 1:
                pair = H // 2
                cp = ACTE.do(lambda e: e.copy(pair_sb[pair % 2][:, :], pv.ap[:, :]), m, g(("pair_tr", pair - 2)))
                pv.free = [cp]
                tails.append(finish_pair(pair, cp))

        def finish_pair(pair, cp):
            b, h = divmod(2 * pair, NHEAD)
            half, n = h // HPH, pair % 2
            bk = side_ring.take()
            for c in range(C):
                m = tr(bk.ap[:, c * P:(c + 1) * P], pair_sb[n][:, c * P:(c + 1) * P], ident[:, :], cp, *bk.free)
            last[("pair_tr", pair)] = m
            turned = bk.ap[:, :].rearrange("p (c i s d) -> p c i s d", c=C, i=2, s=2)
            r = DVE.do(lambda e: e.reciprocal(sum_inv[:, :, :], turned[:, :, :, 1, 0]), m)
            for c in range(C):
                o = DVE.do(lambda e, c=c: e.tensor_tensor(
                    att_q[half][:, c, n, :].rearrange("p (i d) -> p i d", i=2), turned[:, c, :, 0, :],
                    sum_inv[:, c, :].unsqueeze(2).to_broadcast([P, 2, DQ]), ALU.mult), r, g(("att_tr", half)))
            bk.free = [o]
            yield
            if n == 1:
                bk = side_ring.take()
                for c in range(C):
                    m = tr(bk.ap[:, c * P:(c + 1) * P], att_q[half][:, c, :, :].rearrange("p n w -> p (n w)"),
                           ident[:, :], o, *bk.free)
                last[("att_tr", half)] = m
                xb = x_buf[b % NX]
                x3 = DVE.do(lambda e: e.tensor_tensor(xb[:, half, :], bk.ap[:, :], xb[:, half, :], ALU.add), m,
                            ready3[b][3])
                bk.free = [x3]
                attended[(b, half)] = x3
            yield

        out_in = [arrivals(f"out_in{i}") for i in range(NX)]
        sent = [arrivals(f"sent{i}") for i in range(2)]
        sent_mark = [None, None]
        out_marks = [None] * NX

        def dispatch(b):
            xb, rw, si = x_buf[b % NX], rows[b % 2], slot_i[b % 2]
            x3 = [attended[(b, i)] for i in range(HALF)]
            dst = out[b * HALF * P:(b + 1) * HALF * P, :].rearrange("(h p) t -> p h t", p=P)
            out_marks[b % NX] = om = SP.dma(lambda e: e.dma_start(dst, xb[:, :, :]), out_in[b % NX], *x3)
            w = norm_stats(halves(xb), row_stat4, row_mv4, row_rstd4, x3)
            yield
            yield
            xn_ok = norm_apply(halves(xb), halves(rw), row_mv4, row_rstd4, w, sent_mark[b % 2], fill_mark)
            x_free[b % NX] = [om, xn_ok]
            for k in range(HALF):
                no = DVE.do(lambda e, k=k: e.tensor_scalar(rw[:, k, T:T + 1].bitcast(I32), row_no[:, 0:1],
                                                           float((b * HALF + k) * P), None, ALU.add))
            yield
            for k in range(HALF):
                bk = side_ring.take()
                for c in range(C):
                    m = tr(bk.ap[:, c * P:(c + 1) * P], rw[:, k, c * P:(c + 1) * P], ident[:, :], xn_ok, *bk.free)
                t_ok = ACTE.do(lambda e, bk=bk, k=k: e.copy(x_t4[:, k, :, :],
                                                           bk.ap[:, :].rearrange("p (c q) -> p c q", c=C)),
                               m, g("route_mm"))
                bk.free = [t_ok]
                yield
            bk = side_ring.take()
            for k in range(HALF):
                for c in range(C):
                    m = mm(bk.ap[:, k * NEXP:(k + 1) * NEXP], x_t4[:, k, c, :], route_w[:, c, :], c == 0, c == C - 1,
                           t_ok, *bk.free)
            last["route_mm"] = m
            both = bk.ap[:, 0:HALF * NEXP].rearrange("p (k n) -> p k n", k=HALF)
            r = DVE.do(lambda e: e.tensor_reduce(r_max[:, :], both, X, ALU.max), m)
            r = DVE.do(lambda e: e.tensor_scalar(r_max[:, :], r_max[:, :], -1.0, None, ALU.mult), r)
            for k in range(HALF):
                s = ACTE.do(lambda e, bk=bk, k=k: e.activation(r_exp[:, k, :], bk.ap[:, k * NEXP:(k + 1) * NEXP],
                                                              ACT.Exp, bias=r_max[:, k:k + 1],
                                                              accum_out=r_sum[:, k:k + 1]), r)
            bk.free = [s]
            yield
            r = DVE.do(lambda e: e.reciprocal(r_inv[:, :], r_sum[:, :]), s)
            for k in range(HALF):
                pk = DVE.do(lambda e, k=k: e.tensor_scalar(r_exp[:, k, :], r_exp[:, k, :], r_inv[:, k:k + 1], None,
                                                           ALU.mult), r)
            for k in range(HALF):
                t8 = DVE.do(lambda e, k=k: e.max(top8[:, k, :], r_exp[:, k, :]), pk)
            for k in range(HALF):
                rp = DVE.do(lambda e, k=k: e.match_replace(out=repl[:, k, :], in_to_replace=top8[:, k, :],
                                                           in_values=r_exp[:, k, :], imm_value=-1.0), t8)
            s8 = DVE.do(lambda e: e.tensor_reduce(r_top[:, :], top8[:, :, :], X, ALU.add), t8)
            mk = DVE.do(lambda e: e.tensor_scalar(mask[:, :, :], repl[:, :, :], 0.0, None, ALU.is_lt), rp)
            r8 = DVE.do(lambda e: e.reciprocal(r_topi[:, :], r_top[:, :]), s8)
            for k in range(HALF):
                wt = DVE.do(lambda e, k=k: e.tensor_scalar(rw[:, k, T + 1:ROW], r_exp[:, k, :], r_topi[:, k:k + 1],
                                                           None, ALU.mult), r8)
            yield
            bk = side_ring.take()
            for k in range(HALF):
                dst_ap = bk.ap[:, k * NEXP:(k + 1) * NEXP]
                mm(dst_ap, below[:, :], mask[:, k, :], True, False, mk, *bk.free)
                for kk in range(k):
                    mm(dst_ap, ones[:, :], mask[:, kk, :], False, False)
                m = mm(dst_ap, ones[:, :], seen[:, :], False, True, g("seen"))
            for k in range(HALF):
                last["seen"] = DVE.do(lambda e, k=k: e.tensor_tensor(seen[:, :], seen[:, :], mask[:, k, :], ALU.add),
                                      m, last["seen"] if k else None)
            both2 = bk.ap[:, 0:HALF * NEXP].rearrange("p (k n) -> p k n", k=HALF)
            o1 = DVE.do(lambda e: e.tensor_scalar(over[:, :, :], both2, float(CAP), float(2 * NSLOT), ALU.is_ge,
                                                  ALU.mult), m)
            for k in range(HALF):
                o2 = DVE.do(lambda e, bk=bk, k=k: e.tensor_tensor(grid[:, k, :], bk.ap[:, k * NEXP:(k + 1) * NEXP],
                                                                  expert_off[:, :], ALU.add), m)
            bk.free = [o2]
            o = DVE.do(lambda e: e.tensor_tensor(grid[:, :, :], grid[:, :, :], over[:, :, :], ALU.add), o2, o1)
            o = DVE.do(lambda e: e.tensor_tensor(grid[:, :, :], grid[:, :, :], mask[:, :, :], ALU.mult), o)
            for k in range(HALF):
                o5 = DVE.do(lambda e, k=k: e.max(slot8[:, k, :], grid[:, k, :]), o)
            slots_ok = DVE.do(lambda e: e.tensor_scalar(si[:, :, :], slot8[:, :, :], -1.0, None, ALU.add), o5,
                              sent_mark[b % 2])
            yield
            for k in range(HALF):
                for n in range(TOPK):
                    mark = POOL.dma(lambda e, k=k, n=n: e.indirect_dma_start(
                        out=slots_dram, in_=rw[:, k, :], in_offset=None,
                        out_offset=bass.IndirectOffsetOnAxis(ap=si[:, k, n:n + 1].bitcast(U32), axis=0),
                        bounds_check=NSLOT - 1, oob_is_err=False),
                        sent[b % 2], slots_ok, wt, no, xn_ok, fill_mark)
                    yield
            sent_mark[b % 2] = mark

        def piece(gen):
            try:
                next(gen)
                return True
            except StopIteration:
                return False

        def run_all(gen):
            while piece(gen):
                pass

        AHEAD = 2
        SLOTS = NHEAD * C
        load_batch(1)
        run_all(prepare(0))
        for H in range(AHEAD):
            for c in range(C):
                score_chunk(H, c)
        max_rows(0)
        preparing = prepare(1)
        preparing_batch = 1
        dispatching = None
        pending = None
        for n in range(B * SLOTS):
            b, s = divmod(n, SLOTS)
            H, j = divmod(n, C)
            if s == 8 and b + 2 < B:
                load_batch(b + 2)
            if s == SLOTS - AHEAD * C and preparing_batch == b + 1:
                run_all(preparing)
            now = key_chunk(H, j)
            for _ in range(2 if n % 4 == 0 else 1):
                if not piece(preparing) and preparing_batch + 1 < B and preparing_batch + 1 in loaded:
                    preparing_batch += 1
                    preparing = prepare(preparing_batch)
            if H + AHEAD < B * NHEAD:
                score_chunk(H + AHEAD, j)
            if tails and not piece(tails[0]):
                tails.pop(0)
            if pending is not None:
                weighted(*pending)
            pending = now
            if j == 2 and H + 1 < B * NHEAD:
                max_rows(H + 1)
            if s == 5 and b >= 1:
                if dispatching is not None:
                    run_all(dispatching)
                dispatching = dispatch(b - 1)
            if dispatching is not None:
                piece(dispatching)
        weighted(*pending)
        for tail in tails:
            run_all(tail)
        if dispatching is not None:
            run_all(dispatching)
        run_all(dispatch(B - 1))

        end_a = [PE.last, ACTE.last, DVE.last]
        sent_all = [m for m in sent_mark if m is not None]
        small.close()
        NB = 6
        W = lambda name, shape, dt=F32: sb(name, shape, dt)
        gu = [W(f"gate_up{i}", [P, C, 2 * INNER]) for i in range(NB)]
        dn = [W(f"down{i}", [IC, 2, T]) for i in range(NB)]
        xe = [W(f"x_slots{i}", [P, 2, ROW]) for i in range(NB)]
        xet = [W(f"x_slots_t{i}", [P, C, P]) for i in range(3)]
        act_g = [W(f"silu{i}", [P, INNER]) for i in range(2)]
        hid = [W(f"hidden{i}", [P, INNER]) for i in range(2)]
        hid_t = [W(f"hidden_t{i}", [IC, 2, P]) for i in range(2)]
        ye = [W(f"y_slots{i}", [P, 2, T]) for i in range(2)]
        e_in = [arrivals(f"expert_in{i}") for i in range(NB)]
        added = [arrivals(f"added{i}") for i in range(2)]
        xt_ring, gu_ring, ht_ring, y_ring = (Ring(banks[2 * i:2 * i + 2]) for i in range(4))
        e_mark, y_mark, added_mark = {}, {}, [None, None]
        xslot_read, gu_read, dn_read = {}, {}, {}
        SP.wait(*end_a, *sent_all, *[m for m in out_marks if m])

        def load_expert(e_):
            i = e_ % NB
            src = slots_dram[e_ * CAP:(e_ + 1) * CAP, :].rearrange("(c p) w -> p c w", p=P)
            SP.dma(lambda e: e.dma_start(gu[i][:, :, :], a["gate_up"][e_]), e_in[i], gu_read.get(e_ - NB))
            SP.dma(lambda e: e.dma_start(dn[i][:, :, :], a["down"][e_]), e_in[i], dn_read.get(e_ - NB))
            e_mark[e_] = SP.dma(lambda e: e.dma_start(xe[i][:, :, :], src), e_in[i], xslot_read.get(e_ - NB),
                                y_mark.get(e_ - NB))

        st = {}

        def turn(u):
            e_, s = divmod(u, 2)
            i = e_ % NB
            bk = xt_ring.take()
            for c in range(C):
                m = tr(bk.ap[:, c * P:(c + 1) * P], xe[i][:, s, c * P:(c + 1) * P], ident[:, :], e_mark[e_], *bk.free)
            o = DVE.do(lambda e: e.tensor_copy(xet[u % 3][:, :, :], bk.ap[:, :].rearrange("p (c q) -> p c q", c=C)), m,
                       st.get(("gu_mm", u - 3)))
            bk.free = [o]
            st[("xt", u)] = o

        def up(u):
            e_, s = divmod(u, 2)
            i = e_ % NB
            bk = gu_ring.take()
            for c in range(C):
                m = mm(bk.ap[:, 0:2 * INNER], xet[u % 3][:, c, :], gu[i][:, c, :], c == 0, c == C - 1, st[("xt", u)],
                       *bk.free)
            st[("gu_mm", u)] = gu_read[e_] = m
            o = ACTE.do(lambda e: e.activation(act_g[u % 2][:, :], bk.ap[:, 0:INNER], ACT.Silu), m,
                        st.get(("hid", u - 2)))
            h = DVE.do(lambda e: e.tensor_tensor(hid[u % 2][:, :], bk.ap[:, INNER:2 * INNER], act_g[u % 2][:, :],
                                                 ALU.mult), o, st.get(("hid_tr", u - 2)))
            bk.free = [h]
            st[("hid", u)] = h

        def turn_hidden(u):
            bk = ht_ring.take()
            for n in range(2):
                m = tr(bk.ap[0:IC, n * P:(n + 1) * P], hid[u % 2][:, n * IC:(n + 1) * IC], ident[:, :], st[("hid", u)],
                       *bk.free)
            st[("hid_tr", u)] = m
            o = ACTE.do(lambda e: e.copy(hid_t[u % 2][:, :, :], bk.ap[0:IC, 0:2 * P].rearrange("p (n q) -> p n q", n=2)),
                        m, st.get(("y_mm", u - 2)))
            bk.free = [o]
            st[("ht", u)] = o

        def down(u):
            e_, s = divmod(u, 2)
            i = e_ % NB
            bk = y_ring.take()
            for n in range(2):
                m = mm(bk.ap[:, :], hid_t[u % 2][:, n, :], dn[i][:, n, :], n == 0, n == 1, st[("ht", u)], *bk.free)
            st[("y_mm", u)] = dn_read[e_] = m
            o = ACTE.do(lambda e: e.activation(ye[e_ % 2][:, s, :], bk.ap[:, :], ACT.Copy,
                                               scale=xe[i][:, s, T + 1 + e_:T + 2 + e_]), m, added_mark[e_ % 2])
            bk.free = [o]
            st[("y", u)] = xslot_read[e_] = o
            if s == 1:
                prev = y_mark.get(e_ - 1)
                for q in range(2):
                    y_mark[e_] = POOL.dma(lambda e, q=q: e.indirect_dma_start(
                        out=out, out_offset=bass.IndirectOffsetOnAxis(ap=xe[i][:, q, T:T + 1].bitcast(U32), axis=0),
                        in_=ye[e_ % 2][:, q, :], in_offset=None, compute_op=ALU.add),
                        added[e_ % 2], o, st[("y", u - 1)], prev, e_mark[e_])
                added_mark[e_ % 2] = y_mark[e_]

        U = 2 * NEXP
        for e_ in range(min(NB - 2, NEXP)):
            load_expert(e_)
        for line in (DVE, ACTE, PE, POOL):
            line.wait(*end_a)
        for line in (DVE, ACTE):
            line.wait(*sent_all)
        for t in range(-3, U):
            if t >= 0 and t % 2 == 0 and t // 2 + NB - 2 < NEXP:
                load_expert(t // 2 + NB - 2)
            if 0 <= t + 3 < U:
                turn(t + 3)
            if 0 <= t + 2 < U:
                up(t + 2)
            if 0 <= t + 1 < U:
                turn_hidden(t + 1)
            if t >= 0:
                down(t)
        SP.wait(*[m for m in added_mark if m], *[m for m in out_marks if m], fill_mark, *sent_all)

        lines = (("tensor", PE), ("vector", DVE), ("scalar", ACTE), ("gpsimd", POOL), ("sync", SP))
        for _, line in lines:
            line.number()
        block = stack.enter_context(nc.Block())

        @block.tensor
        def _(e):
            PE.play(e)

        @block.vector
        def _(e):
            DVE.play(e)

        @block.scalar
        def _(e):
            ACTE.play(e)

        @block.gpsimd
        def _(e):
            POOL.play(e)

        @block.sync
        def _(e):
            SP.play(e)


def kernel(x, ctx_2048, L0_xattn_theta_w, L0_xattn_theta_b, L0_xattn_phi_w, L0_xattn_phi_b, L0_xattn_g_w,
           L0_xattn_g_b, L0_xattn_ln_gamma, L0_xattn_ln_beta, L0_xattn_out_w, L0_xattn_out_b, L0_ffn_W_base,
           L0_ffn_b_base, L0_ffn_W_router, L0_ffn_A_w, L0_ffn_B_w, L1_xattn_gamma, L1_ffn_router_weight,
           L1_ffn_gate_proj, L1_ffn_up_proj, L1_ffn_down_proj):
    import concourse.bacc as _bacc
    from concourse.bass_utils import run_bass_kernel_spmd as _run

    n = np.asarray
    B, rows, T = x.shape
    HALF = rows // P
    NE, NRANK, _ = L0_ffn_A_w.shape
    NEXP, D, INNER = L1_ffn_gate_proj.shape
    dims = dict(B=B, HALF=HALF, T=T, L=L0_xattn_theta_w.shape[0], NHEAD=8, DQ=rows // 8, NE=NE, NRANK=NRANK,
                NEXP=NEXP, CAP=2 * (2 * 512 * 8) // NEXP, TOPK=8, INNER=INNER, LORA_SCALE=16.0 / NRANK)
    CAP = dims["CAP"]
    gate_up = np.concatenate([n(L1_ffn_gate_proj), n(L1_ffn_up_proj)], axis=2)
    gate_up = gate_up.reshape(NEXP, D // P, P, 2 * INNER).transpose(0, 2, 1, 3)
    down = n(L1_ffn_down_proj).reshape(NEXP, 2, INNER // 2, D).transpose(0, 2, 1, 3)
    arrays = {
        "x": n(x), "ctx": n(ctx_2048),
        "theta_wT": n(L0_xattn_theta_w).T, "phi_wT": n(L0_xattn_phi_w).T, "g_wT": n(L0_xattn_g_w).T,
        "lat_b": np.stack([n(L0_xattn_theta_b), n(L0_xattn_phi_b), n(L0_xattn_g_b)], axis=1),
        "ln_gamma": n(L0_xattn_ln_gamma), "ln_beta": n(L0_xattn_ln_beta),
        "out_wT": n(L0_xattn_out_w).T, "out_b": n(L0_xattn_out_b).reshape(HALF, P).T,
        "base_wT": n(L0_ffn_W_base).T,
        "lora_in": np.concatenate([n(L0_ffn_W_router), n(L0_ffn_A_w).reshape(NE * NRANK, T)], axis=0).T,
        "lora_out": np.concatenate([n(L0_ffn_B_w).transpose(0, 2, 1).reshape(NE * NRANK, T),
                                    n(L0_ffn_b_base).reshape(1, T)], axis=0),
        "route_w": n(L1_ffn_router_weight),
        "gamma1": np.broadcast_to(n(L1_xattn_gamma).reshape(1, 1), (P, 1)),
        "gate_up": gate_up, "down": down,
    }
    arrays = {f"in_{k}": np.ascontiguousarray(v) for k, v in arrays.items()}
    nc = _bacc.Bacc("TRN2", target_bir_lowering=False, num_devices=1)
    aps = {k[3:]: nc.dram_tensor(k, v.shape, mybir.dt.from_np(v.dtype), kind="ExternalInput").ap()
           for k, v in arrays.items()}
    out = nc.dram_tensor("out_rows", (B * rows + CAP, T), F32, kind="ExternalOutput").ap()
    slots = nc.dram_tensor("slot_rows", (NEXP * CAP, T + 1 + NEXP), F32, kind="Internal").ap()
    build(nc, aps, out, slots, dims)
    r = _run(nc, [arrays], core_ids=[0])
    return r.results[0]["out_rows"][:B * rows].reshape(B, rows, T)
```

```python
from contextlib import ExitStack

import numpy as np

import concourse.bass as bass
from concourse import mybir

ALU = mybir.AluOpType
ACT = mybir.ActivationFunctionType
X = mybir.AxisListType.X
F32 = mybir.dt.float32
F32R = mybir.dt.float32r
I32 = mybir.dt.int32
U32 = mybir.dt.uint32

P = 128
EPS = 1e-5


class Step:

    def __init__(self, line, run):
        self.line, self.run, self.waited, self.count = line, run, False, None


class Line:

    def __init__(self, sem):
        self.sem, self.items = sem, []

    def wait(self, *steps):
        for s in steps:
            if s is not None:
                s.waited = True
                self.items.append(("wait", s))

    def do(self, run, *after):
        self.wait(*after)
        self.last = Step(self, run)
        self.items.append(("do", self.last))
        return self.last

    def dma(self, run, done, *after):
        self.wait(*after)
        mark = done.next()
        self.items.append(("dma", (run, done.sem)))
        return mark

    def number(self):
        n = 0
        for kind, s in self.items:
            if kind == "do" and s.waited:
                n += 1
                s.count = n

    def play(self, engine):
        reached = {}
        for kind, s in self.items:
            if kind == "wait":
                sem, count = (s.line.sem, s.count) if isinstance(s, Step) else (s.sem, s.count)
                if reached.get(id(sem), 0) < count:
                    engine.wait_ge(sem, count)
                    reached[id(sem)] = count
            elif kind == "do":
                ins = s.run(engine)
                if s.waited:
                    ins.then_inc(self.sem, 1)
            else:
                s[0](engine).then_inc(s[1], 16)


class Mark:
    def __init__(self, sem, count):
        self.sem, self.count, self.waited = sem, count, True


class Arrivals:

    def __init__(self, sem):
        self.sem, self.count = sem, 0

    def next(self):
        self.count += 16
        return Mark(self.sem, self.count)


class Bank:

    def __init__(self, ap):
        self.ap, self.free = ap, []


class Ring:
    def __init__(self, banks):
        self.banks, self.n = banks, 0

    def take(self):
        self.n += 1
        return self.banks[(self.n - 1) % len(self.banks)]


def build(nc, a, out, slots_dram, dims):
    B, HALF, T, L, NHEAD, DQ, NE, NEXP, CAP, TOPK, NRANK = (
        dims[k] for k in ("B", "HALF", "T", "L", "NHEAD", "DQ", "NE", "NEXP", "CAP", "TOPK", "NRANK"))
    C = T // P
    NR = NE * NRANK
    NF = NR + 1
    ROWS = B * HALF * P
    INNER = dims["INNER"]
    IC = INNER // 2
    ROW = T + 1 + NEXP
    NSLOT = NEXP * CAP
    SCALE = float(DQ) ** -0.5
    SK = 3 * DQ
    SKM = SK + 2
    HPH = NHEAD // HALF

    stack = ExitStack()
    with stack:
        def sem(name):
            return stack.enter_context(nc.semaphore(name))

        def sb(name, shape, dt=F32, on=stack):
            return on.enter_context(nc.sbuf_tensor(name, shape, dt))

        PE, DVE, ACTE, POOL, SP = (Line(sem(n)) for n in ("pe_done", "dve_done", "act_done", "pool_done", "sp_done"))

        def arrivals(name):
            return Arrivals(sem(name))

        psum = [stack.enter_context(nc.psum_tensor(f"bank{i}", [P, 512], F32)) for i in range(8)]
        banks = [Bank(t) for t in psum]

        def mm(bank_ap, lhsT, rhs, start, stop, *after):
            return PE.do(lambda e: e.matmul(bank_ap, lhsT, rhs, start=start, stop=stop), *after)

        def tr(bank_ap, src, ident_ap, *after):
            return PE.do(lambda e: e.transpose(bank_ap, src, ident_ap), *after)

        small = ExitStack()
        stack.enter_context(small)
        ident = sb("ident", [P, P])
        ones = sb("ones", [P, P])
        rows = [sb(f"row{i}", [P, HALF, ROW]) for i in range(2)]
        slot_i = [sb(f"slot_i{i}", [P, HALF, TOPK], I32) for i in range(2)]

        def A(name, shape, dt=F32):
            return sb(name, shape, dt, small)

        below = A("below", [P, P])
        mean_w = A("mean_w", [P, P])
        neg_half = A("neg_half", [P, 2])
        iota8 = A("iota8", [P, NE])
        expert_off = A("expert_off", [P, NEXP])
        row_no = A("row_no", [P, 2])
        theta_w = A("theta_w", [P, HALF, L])
        phi_w = A("phi_w", [P, HALF, L])
        g_w = A("g_w", [P, HALF, L])
        lat_b = A("lat_b", [P, 3])
        ln_gamma = A("ln_gamma", [P, T])
        ln_beta = A("ln_beta", [P, T])
        out_w = A("out_w", [P, HALF * P])
        out_b = A("out_b", [P, HALF])
        base_w = A("base_w", [P, C, T])
        lora_in = A("lora_in", [P, C, NE + NR])
        lora_out = A("lora_out", [NF, T])
        route_w = A("route_w", [P, C, NEXP])
        gamma1 = A("gamma1", [P, 1])
        fill_row = rows[0]

        weights_in = arrivals("weights_in")

        def load(dst, src):
            return SP.dma(lambda e: e.dma_start(dst, src), weights_in)

        NX = 4
        x_buf = [A(f"x{i}", [P, HALF, T]) for i in range(NX)]
        ctx_buf = [A(f"ctx{i}", [P, HALF, T]) for i in range(2)]
        x_in = [arrivals(f"x_in{i}") for i in range(NX)]
        ctx_in = [arrivals(f"ctx_in{i}") for i in range(2)]
        x_free, ctx_free = [[] for _ in range(NX)], [[], []]
        loaded = {}

        def load_batch(b):
            xb, cb = x_buf[b % NX], ctx_buf[b % 2]
            mx = SP.dma(lambda e: e.dma_start(xb[:, :, :], a["x"][b].rearrange("(h p) t -> p h t", p=P)),
                        x_in[b % NX], *x_free[b % NX])
            mc = SP.dma(lambda e: e.dma_start(cb[:, :, :], a["ctx"][b].rearrange("(h p) t -> p h t", p=P)),
                        ctx_in[b % 2], *ctx_free[b % 2])
            loaded[b] = (mx, mc)

        load_batch(0)
        for h in range(HALF):
            load(theta_w[:, h, :], a["theta_wT"][h * P:(h + 1) * P, :])
            load(phi_w[:, h, :], a["phi_wT"][h * P:(h + 1) * P, :])
            load(g_w[:, h, :], a["g_wT"][h * P:(h + 1) * P, :])
        load(lat_b[:, :], a["lat_b"])
        load(ln_gamma[:, :], a["ln_gamma"])
        load(ln_beta[:, :], a["ln_beta"])
        load(out_w[:, :], a["out_wT"])
        load(out_b[:, :], a["out_b"])
        load(base_w[:, :, :], a["base_wT"].rearrange("(c p) o -> p c o", p=P))
        load(lora_in[:, :, :], a["lora_in"].rearrange("(c p) o -> p c o", p=P))
        load(lora_out[:, :], a["lora_out"])
        load(route_w[:, :, :], a["route_w"].rearrange("(c p) o -> p c o", p=P))
        weights_ready = load(gamma1[:, :], a["gamma1"])

        q_st = [A(f"q_stack{i}", [SKM, NHEAD, T], F32R) for i in range(2)]
        k_st = [A(f"k_stack{i}", [SKM, NHEAD, T], F32R) for i in range(2)]
        VW = 3 * DQ
        v_t = [A(f"v_t{i}", [P, C, NHEAD, VW], F32R) for i in range(2)]
        fold = A("fold", [VW, 2 * DQ])
        max_col = A("max_col", [P, C, SKM])

        m0 = POOL.do(lambda e: e.memset(ident[:, :], 0.0))
        ident_ok = POOL.do(lambda e: e.affine_select(out=ident[:, :], in_=ident[:, :], compare_op=ALU.not_equal,
                                                     fill=1.0, base=0, pattern=[[-1, P]], channel_multiplier=1), m0)
        ones_ok = POOL.do(lambda e: e.memset(ones[:, :], 1.0))
        mw_ok = POOL.do(lambda e: e.memset(mean_w[:, :], 1.0 / P))
        below_ok = POOL.do(lambda e: e.affine_select(out=below[:, :], in_=ones[:, :], compare_op=ALU.is_gt, fill=0.0,
                                                     base=0, pattern=[[1, P]], channel_multiplier=-1), ones_ok)
        POOL.do(lambda e: e.memset(neg_half[:, :], -0.5))
        POOL.do(lambda e: e.iota(iota8[:, :], pattern=[[1, NE]], base=0, channel_multiplier=0,
                                 allow_small_or_imprecise_dtypes=True))
        POOL.do(lambda e: e.iota(expert_off[:, :], pattern=[[CAP, NEXP]], base=1, channel_multiplier=0,
                                 allow_small_or_imprecise_dtypes=True))
        f0 = POOL.do(lambda e: e.memset(fill_row[:, :, :], 0.0))
        for c in range(2):
            dst = fill_row[:, c, T:T + 1].bitcast(I32)
            fill_ok = POOL.do(lambda e, d=dst, c=c: e.iota(d, pattern=[[0, 1]], base=ROWS + c * P,
                                                           channel_multiplier=1), f0)
        rn = POOL.do(lambda e: e.iota(row_no[:, :], pattern=[[P, 2]], base=0, channel_multiplier=1,
                                      allow_small_or_imprecise_dtypes=True))
        POOL.do(lambda e: e.memset(max_col[:, :, :], 0.0))
        for i in range(2):
            v_ones = POOL.do(lambda e, t=v_t[i]: e.memset(t[:, :, :, :].bitcast(F32), 1.0))
            k_ones = DVE.do(lambda e, t=k_st[i]: e.memset(t[SK:SKM, :, :].bitcast(F32), 1.0))

        fz = DVE.do(lambda e: e.memset(fold[:, :], 0.0))
        f1 = DVE.do(lambda e: e.tensor_copy(fold[0:DQ, 0:DQ], ident[0:DQ, 0:DQ]), fz, ident_ok)
        f2 = DVE.do(lambda e: e.tensor_copy(fold[DQ:2 * DQ, 0:DQ], ident[0:DQ, 0:DQ]), fz, ident_ok)
        fold_ok = DVE.do(lambda e: e.tensor_copy(fold[2 * DQ:3 * DQ, DQ:2 * DQ], ident[0:DQ, 0:DQ]), fz, ident_ok)

        slots_filled = arrivals("slots_filled")

        def fill(e_):
            d = slots_dram[e_ * CAP:(e_ + 1) * CAP, :].rearrange("(c p) w -> p c w", p=P)
            return SP.dma(lambda e: e.dma_start(d, fill_row[:, :, :]), slots_filled, fill_ok, f0)

        spare = out[ROWS:ROWS + CAP, :].rearrange("(c p) t -> p c t", p=P)
        SP.dma(lambda e: e.dma_start(spare, fill_row[:, :, 0:T]), slots_filled, fill_ok, f0)
        filled = []

        xn = A("xn", [P, HALF, T])
        theta = A("theta", [P, T])
        phi = A("phi", [P, T])
        g_sb = A("g_sb", [P, T])
        prob = A("prob", [P, C, T])
        prob_t = A("prob_t", [P, C, T])
        lat = A("lat", [P, T])
        x_t4 = A("x_t4", [P, HALF, C, P])
        hi, lo = prob[:, 0:HALF, :].bitcast(F32R), prob[:, HALF:2 * HALF, :].bitcast(F32R)
        x_t = prob_t[:, 0:HALF, :].rearrange("p k (c q) -> p k c q", c=C)
        row_stat = A("row_stat", [P, HALF, 6])
        row_mv = A("row_mv", [P, HALF, 2])
        row_rstd = A("row_rstd", [P, HALF])
        x_stat = A("x_stat", [P, HALF, 6])
        x_mv = A("x_mv", [P, HALF, 2])
        x_rstd = A("x_rstd", [P, HALF])
        row_stat4 = A("row_stat4", [P, HALF, 6])
        row_mv4 = A("row_mv4", [P, HALF, 2])
        row_rstd4 = A("row_rstd4", [P, HALF])
        lat_stat = A("lat_stat", [P, 6])
        lat_mv = A("lat_mv", [P, 2])
        lat_mom = A("lat_mom", [P, 2])
        lat_all = A("lat_all", [P, 4])
        neg_max = A("neg_max", [P, C])
        exp_sum = A("exp_sum", [P, C])
        lora_mid = A("lora_mid", [P, HALF, NE + NR])
        top2 = A("top2", [P, HALF, 8])
        top2_at = A("top2_at", [P, HALF, 8], U32)
        top2_f = A("top2_f", [P, HALF, 2])
        gate_s = A("gate_s", [P, 4, HALF])
        gate_2 = A("gate_2", [P, HALF, 2])
        gate = A("gate", [P, HALF, 2, NE])
        gated = A("gated", [P, HALF, NF])
        gated_t = A("gated_t", [NF, HALF, P])
        p_all = [A(f"p_all{i}", [P, T]) for i in range(2)]
        PARTS = 3
        p_hi = [A(f"p_hi{i}", [P, T], F32R) for i in range(PARTS)]
        p_lo = [A(f"p_lo{i}", [P, T], F32R) for i in range(PARTS)]
        q_max = [A(f"q_max{i}", [P, C]) for i in range(2)]
        head_sb = [A(f"head_sb{i}", [VW, T]) for i in range(2)]
        sum_inv = A("sum_inv", [P, 2, C])
        att_q = [A(f"att_q{i}", [P, C, 2, 2 * DQ]) for i in range(2)]
        r_max = A("r_max", [P, HALF])
        r_sum = A("r_sum", [P, HALF])
        r_inv = A("r_inv", [P, HALF])
        r_top = A("r_top", [P, HALF])
        r_topi = A("r_topi", [P, HALF])
        r_exp = A("r_exp", [P, HALF, NEXP])
        top8 = A("top8", [P, HALF, TOPK])
        repl = A("repl", [P, HALF, NEXP])
        mask = A("mask", [P, HALF, NEXP])
        seen = A("seen", [P, NEXP])
        over = A("over", [P, HALF, NEXP])
        grid = A("grid", [P, HALF, NEXP])
        slot8 = A("slot8", [P, HALF, TOPK])

        gated_one = DVE.do(lambda e: e.memset(gated[:, :, :], 1.0))
        seen_ok = DVE.do(lambda e: e.memset(seen[:, :], 0.0))
        for line in (PE, ACTE, DVE, POOL):
            line.wait(weights_ready, k_ones, v_ones, fold_ok, f1, f2, ident_ok, below_ok, mw_ok, rn,
                      gated_one, seen_ok)

        s_ring, st_ring, pv_ring = Ring(banks[0:2]), Ring(banks[2:4]), Ring(banks[4:5])
        prep_ring, side_ring = Ring(banks[5:7]), Ring(banks[7:8])
        last = {}
        g = last.get

        def norm_stats(src, st, m, r, ready):
            for i in range(HALF):
                s = DVE.do(lambda e, i=i: e.bn_stats(st[:, i, :], src[i]), *ready)
                agg = DVE.do(lambda e, i=i: e.bn_aggr(m[:, i, :], st[:, i, :]), s)
            v = POOL.do(lambda e: e.tensor_scalar(r[:, :], m[:, :, 1], EPS, None, ALU.add), agg)
            return POOL.do(lambda e: e.tensor_tensor(r[:, :], r[:, :], neg_half[:, :], ALU.pow), v)

        def norm_apply(src, dst, m, r, *after):
            for i in range(HALF):
                o = DVE.do(lambda e, i=i: e.tensor_scalar(dst[i], src[i], m[:, i, 0:1], r[:, i:i + 1],
                                                          ALU.subtract, ALU.mult), *after)
            return o

        def halves(t):
            return [t[:, i, 0:T] for i in range(HALF)]

        heads_done = []
        operands_of = {}
        k_in = [arrivals(f"k_in{i}") for i in range(2)]
        q_in = [arrivals(f"q_in{i}") for i in range(2)]

        x_stats = {}

        def first_stats(b):
            x_stats[b] = norm_stats(halves(x_buf[b % NX]), x_stat, x_mv, x_rstd, [loaded[b][0], g("x_normed")])

        def prepare(b):
            xb, cb = x_buf[b % NX], ctx_buf[b % 2]
            _, c_ok = loaded[b]

            def split_hi(src, src_ok):
                return ACTE.do(lambda e: e.copy(hi, src), src_ok, g("stacked"), g("prob_tr"))

            def stack_rows(dst, part, places, done, *after):
                for n in places:
                    for hq in range(HPH):
                        last["stacked"] = SP.dma(lambda e, n=n, hq=hq: e.dma_start(
                            dst[n * DQ:(n + 1) * DQ, hq:NHEAD:HPH, :].bitcast(F32),
                            part[hq * DQ:(hq + 1) * DQ].bitcast(F32)),
                            done, g(("s_mm", b - 2)), g(("st_mm", b - 2)), *after)
                return last["stacked"]

            def split_lo(src, h_ok):
                return DVE.do(lambda e: e.tensor_tensor(lo, src, hi.bitcast(F32), ALU.subtract),
                              h_ok, stacked)

            def values(j2):
                bk = prep_ring.take()
                for j in range(2):
                    for k in range(HALF):
                        m = tr(bk.ap[:, (j * HALF + k) * P:(j * HALF + k + 1) * P],
                               cb[:, k, (2 * j2 + j) * P:(2 * j2 + j + 1) * P], ident[:, :], c_ok, *bk.free)
                src = bk.ap[:, :].rearrange("p (j h d) -> p j h d", j=2, d=DQ)
                vj = v_t[b % 2][:, 2 * j2:2 * j2 + 2]
                s = ACTE.do(lambda e: e.activation(vj[:, :, :, 0:DQ], src, ACT.Copy, scale=gamma1[:, 0:1]), m,
                            g(("pv_mm", b - 2)))
                s = DVE.do(lambda e: e.scalar_tensor_tensor(
                    out=vj[:, :, :, DQ:2 * DQ], in0=src, scalar=gamma1[:, 0:1],
                    in1=vj[:, :, :, 0:DQ].bitcast(F32), op0=ALU.mult, op1=ALU.subtract), s)
                bk.free = [s]
                return s, m

            def project(wt, src, dst, col, rdy):
                bk = prep_ring.take()
                for k in range(HALF):
                    m = mm(bk.ap[:, :], wt[:, k, :], src[:, k, :], k == 0, k == HALF - 1, rdy, *bk.free)
                s = ACTE.do(lambda e: e.activation(dst[:, :], bk.ap[:, :], ACT.Identity, bias=lat_b[:, col:col + 1]),
                            m, g("scores_mm"))
                bk.free = [s]
                return s
            last["x_normed"] = xn_ok = norm_apply(halves(xb), halves(xn), x_mv, x_rstd, x_stats[b], g("xn_read"))
            th_ok = project(theta_w, cb, theta, 0, c_ok)
            yield
            phi_ok = project(phi_w, xn, phi, 1, xn_ok)
            res_ok = [None, None]

            def residual(k):
                res_ok[k] = POOL.do(lambda e: e.tensor_tensor(xb[:, k, :], xb[:, k, :], cb[:, k, :], ALU.add),
                                    xn_ok, c_ok)
            residual(0)
            yield
            bk = prep_ring.take()
            for c in range(C):
                for k in range(HALF):
                    m = mm(bk.ap[:, c * P:(c + 1) * P], xn[:, k, c * P:(c + 1) * P], g_w[:, k, :], k == 0,
                           k == HALF - 1, *bk.free)
            xn_read = m
            g_ok = ACTE.do(lambda e, bk=bk: e.copy(g_sb[:, :], bk.ap[:, :]), m, g("lat_mm"))
            bk.free = [g_ok]
            residual(1)
            yield
            for c in range(C):
                bk = prep_ring.take()
                m = mm(bk.ap[:, :], theta[:, c * P:(c + 1) * P], phi[:, :], True, True, th_ok, phi_ok, *bk.free)
                r = DVE.do(lambda e, bk=bk, c=c: e.tensor_reduce(neg_max[:, c:c + 1], bk.ap[:, :], X, ALU.max), m,
                           g("latent_exp"))
                r = DVE.do(lambda e, c=c: e.tensor_scalar(neg_max[:, c:c + 1], neg_max[:, c:c + 1], -1.0, None,
                                                          ALU.mult), r)
                s = ACTE.do(lambda e, bk=bk, c=c: e.activation(prob[:, c, :], bk.ap[:, :], ACT.Exp,
                                                              bias=neg_max[:, c:c + 1], accum_out=exp_sum[:, c:c + 1]),
                            r, g("prob_tr"), g("exp_sum_read"), g("stacked"))
                bk.free = [s]
                if c < C - 1:
                    yield c == 0
            last["scores_mm"], last["latent_exp"] = m, s
            r = DVE.do(lambda e: e.reciprocal(exp_sum[:, :], exp_sum[:, :]), s)
            norm = [DVE.do(lambda e, c=c: e.tensor_scalar(prob[:, c, :], prob[:, c, :], exp_sum[:, c:c + 1],
                                                          None, ALU.mult), r) for c in range(C)]
            last["exp_sum_read"] = norm[-1]
            yield
            yield
            for j in range(C):
                bk = prep_ring.take()
                for c in range(C):
                    m = tr(bk.ap[:, c * P:(c + 1) * P], prob[:, c, j * P:(j + 1) * P], ident[:, :], norm[c], *bk.free)
                s = ACTE.do(lambda e, bk=bk, j=j: e.copy(prob_t[:, j, :], bk.ap[:, :]), m, g("lat_mm"), g("ffn_mm"))
                bk.free = [s]
                if j % 2:
                    yield
            last["prob_tr"] = m
            while len(heads_done) < (b - 1) * NHEAD:
                yield
            values(0)
            yield True
            bk = prep_ring.take()
            for j in range(C):
                m = mm(bk.ap[:, :], g_sb[:, j * P:(j + 1) * P], prob_t[:, j, :], j == 0, j == C - 1, s, g_ok, *bk.free)
            last["lat_mm"] = m
            s = DVE.do(lambda e, bk=bk: e.tensor_scalar(lat[:, :], bk.ap[:, :], lat_b[:, 2:3], None, ALU.add),
                       m, g("out_mm"))
            bk.free = [s]
            s = DVE.do(lambda e: e.bn_stats(lat_stat[:, :], lat[:, :]), s)
            s = DVE.do(lambda e: e.bn_aggr(lat_mv[:, :], lat_stat[:, :]), s)
            cp = DVE.do(lambda e: e.tensor_copy(lat_mom[:, 0:1], lat_mv[:, 0:1]), s)
            sq = DVE.do(lambda e: e.scalar_tensor_tensor(out=lat_mom[:, 1:2], in0=lat_mv[:, 0:1],
                                                         scalar=lat_mv[:, 0:1], in1=lat_mv[:, 1:2],
                                                         op0=ALU.mult, op1=ALU.add), s)
            yield
            bk = prep_ring.take()
            m = mm(bk.ap[:, 0:2], mean_w[:, :], lat_mom[:, :], True, True, sq, cp, *bk.free)
            cp = DVE.do(lambda e, bk=bk: e.tensor_copy(lat_all[:, 0:2], bk.ap[:, 0:2]), m)
            bk.free = [cp]
            v = DVE.do(lambda e: e.scalar_tensor_tensor(out=lat_all[:, 2:3], in0=lat_all[:, 0:1],
                                                        scalar=lat_all[:, 0:1], in1=lat_all[:, 1:2],
                                                        op0=ALU.mult, op1=ALU.subtract), cp)
            v = POOL.do(lambda e: e.tensor_scalar(lat_all[:, 3:4], lat_all[:, 2:3], -1.0, EPS, ALU.mult, ALU.add), v)
            v = POOL.do(lambda e: e.tensor_tensor(lat_all[:, 3:4], lat_all[:, 3:4], neg_half[:, 0:1], ALU.pow), v)
            stacked = g("stacked")
            h_ok = split_hi(cb[:, :, :], c_ok)
            stack_rows(k_st[b % 2], hi, (0, 1), k_in[b % 2], h_ok)
            yield
            n = DVE.do(lambda e: e.scalar_tensor_tensor(out=lat[:, :], in0=lat[:, :], scalar=lat_all[:, 0:1],
                                                        in1=ln_gamma[:, :], op0=ALU.subtract, op1=ALU.mult), v)
            n = DVE.do(lambda e: e.scalar_tensor_tensor(out=lat[:, :], in0=lat[:, :], scalar=lat_all[:, 3:4],
                                                        in1=ln_beta[:, :], op0=ALU.mult, op1=ALU.add), n)
            n = ACTE.do(lambda e: e.activation(lat[:, :], lat[:, :], ACT.Relu), n)
            yield
            k_read = split_lo(cb[:, :, :], h_ok)
            ks_ok = stack_rows(k_st[b % 2], lo, (2,), k_in[b % 2], k_read)
            vt_ok, ctx_tr = values(1)
            yield
            for k in range(HALF):
                bk = prep_ring.take()
                m = mm(bk.ap[:, :], out_w[:, k * P:(k + 1) * P], lat[:, :], True, True, n, *bk.free)
                x1 = DVE.do(lambda e, bk=bk, k=k: e.scalar_tensor_tensor(
                    out=xb[:, k, :], in0=bk.ap[:, :], scalar=out_b[:, k:k + 1], in1=xb[:, k, :],
                    op0=ALU.add, op1=ALU.add), m, res_ok[k])
                bk.free = [x1]
            last["out_mm"] = m
            ctx_free[b % 2] = [k_read, ctx_tr, res_ok[1]]
            w = norm_stats(halves(xb), row_stat, row_mv, row_rstd, [x1])
            yield
            yield
            xn_ok = norm_apply(halves(xb), halves(xn), row_mv, row_rstd, w, xn_read)
            yield
            yield
            for k in range(HALF):
                bk = prep_ring.take()
                for c in range(C):
                    m = tr(bk.ap[:, c * P:(c + 1) * P], xn[:, k, c * P:(c + 1) * P], ident[:, :], xn_ok, *bk.free)
                t_ok = ACTE.do(lambda e, bk=bk, k=k: e.copy(x_t[:, k, :, :],
                                                           bk.ap[:, :].rearrange("p (c q) -> p c q", c=C)),
                               m, g("ffn_mm"), g("lat_mm"))
                bk.free = [t_ok]
            xn_read = m
            yield
            bk = prep_ring.take()
            W1 = NE + NR
            for k in range(HALF):
                for c in range(C):
                    m = mm(bk.ap[:, k * W1:(k + 1) * W1], x_t[:, k, c, :], lora_in[:, c, :], c == 0, c == C - 1,
                           t_ok, *bk.free)
            r = DVE.do(lambda e, bk=bk: e.tensor_copy(
                lora_mid[:, :, :], bk.ap[:, 0:HALF * W1].rearrange("p (k w) -> p k w", k=HALF)), m)
            bk.free = [r]
            for k in range(HALF):
                t2 = DVE.do(lambda e, k=k: e.max(top2[:, k, :], lora_mid[:, k, 0:NE]), r)
                i2 = DVE.do(lambda e, k=k: e.max_index(top2_at[:, k, :], top2[:, k, :], lora_mid[:, k, 0:NE]), t2)
            d = DVE.do(lambda e: e.tensor_tensor(gate_s[:, 0, :], top2[:, :, 1], top2[:, :, 0], ALU.subtract), t2)
            e1 = ACTE.do(lambda e: e.activation(gate_s[:, 1, :], gate_s[:, 0, :], ACT.Exp), d)
            f = DVE.do(lambda e: e.tensor_copy(top2_f[:, :, :], top2_at[:, :, 0:2]), i2)
            yield
            r = DVE.do(lambda e: e.tensor_scalar(gate_s[:, 2, :], gate_s[:, 1, :], 1.0, 1.0 / dims["LORA_SCALE"],
                                                 ALU.add, ALU.mult), e1)
            r = DVE.do(lambda e: e.reciprocal(gate_2[:, :, 0], gate_s[:, 2, :]), r)
            r = DVE.do(lambda e: e.tensor_tensor(gate_2[:, :, 1], gate_2[:, :, 0], gate_s[:, 1, :], ALU.mult), r)
            for k in range(HALF):
                for n in range(2):
                    q = DVE.do(lambda e, k=k, n=n: e.tensor_scalar(gate[:, k, n, :], iota8[:, :],
                                                                   top2_f[:, k, n:n + 1], gate_2[:, k, n:n + 1],
                                                                   ALU.is_equal, ALU.mult), r, f)
            q = DVE.do(lambda e: e.tensor_tensor(gate[:, :, 0, :], gate[:, :, 0, :], gate[:, :, 1, :], ALU.add), q)
            for k in range(HALF):
                q2 = DVE.do(lambda e, k=k: e.tensor_tensor(
                    gated[:, k, 0:NR].rearrange("p (n r) -> p n r", r=NRANK),
                    lora_mid[:, k, NE:NE + NR].rearrange("p (n r) -> p n r", r=NRANK),
                    gate[:, k, 0, :].unsqueeze(2).to_broadcast([P, NE, NRANK]), ALU.mult), q, g("gated_tr"))
            yield

            def base(bk, k, cs):
                for c in cs:
                    m = mm(bk.ap[:, :], x_t[:, k, c, :], base_w[:, c, :], c == 0, False, *bk.free)
                return m

            def ffn_out(bk, k):
                m = mm(bk.ap[:, :], gated_t[:, k, :], lora_out[:, :], False, True, gt)
                x2 = DVE.do(lambda e: e.tensor_tensor(xb[:, k, :], bk.ap[:, :], xb[:, k, :], ALU.add), m)
                bk.free = [x2]
                return m, x2

            b0 = prep_ring.take()
            base(b0, 0, (0, 1))
            yield
            bk = prep_ring.take()
            for k in range(HALF):
                m = tr(bk.ap[0:NF, k * P:(k + 1) * P], gated[:, k, :], ident[:, :], q2, *bk.free)
            last["gated_tr"] = m
            gt = ACTE.do(lambda e: e.copy(gated_t[:, :, :],
                                          bk.ap[0:NF, 0:HALF * P].rearrange("p (k q) -> p k q", k=HALF)),
                         m, g("ffn_mm"))
            bk.free = [gt]
            base(b0, 0, (2,))
            yield
            base(b0, 0, (3,))
            ffn_out(b0, 0)
            yield
            b1 = prep_ring.take()
            base(b1, 1, (0, 1))
            yield
            base(b1, 1, (2, 3))
            yield
            m, x2 = ffn_out(b1, 1)
            last["ffn_mm"] = m
            w = norm_stats(halves(xb), row_stat, row_mv, row_rstd, [x2])
            yield
            yield
            xn_ok = norm_apply(halves(xb), halves(xn), row_mv, row_rstd, w, xn_read)
            yield
            stacked = g("stacked")
            h_ok = split_hi(xn[:, :, :], xn_ok)
            stack_rows(q_st[b % 2], hi, (0, 2), q_in[b % 2], h_ok)
            yield True
            last["xn_read"] = q_read = split_lo(xn[:, :, :], h_ok)
            qs_ok = stack_rows(q_st[b % 2], lo, (1,), q_in[b % 2], q_read)
            operands_of[b] = (qs_ok, ks_ok, vt_ok, x2)

        all_free, hi_free, lo_free = [None] * 2, [None] * PARTS, [None] * PARTS
        attended, rows_ok, col_ok = {}, {}, {}
        tails = []

        def score_chunk(H, c):
            b, h = divmod(H, NHEAD)
            qs_ok, ks_ok, _, _ = operands_of[b]
            bk = s_ring.take()
            m = mm(bk.ap[:, :], q_st[b % 2][0:SK, h, c * P:(c + 1) * P], k_st[b % 2][0:SK, h, :], True, True,
                   qs_ok, ks_ok, *bk.free)
            last[("s_mm", b)] = m
            r = DVE.do(lambda e: e.tensor_reduce(q_max[H % 2][:, c:c + 1], bk.ap[:, :], X, ALU.max), m)
            bk.free = [r]
            if c == C - 1:
                mc = max_col
                m1 = DVE.do(lambda e: e.tensor_scalar(mc[:, :, SK].bitcast(F32R), q_max[H % 2][:, :], -1.0, None,
                                                      ALU.mult), r, g("mc_tr"))
                col_ok[H] = DVE.do(lambda e: e.scalar_tensor_tensor(out=mc[:, :, SK + 1], in0=q_max[H % 2][:, :],
                                                                    scalar=-1.0, in1=mc[:, :, SK], op0=ALU.mult,
                                                                    op1=ALU.subtract), m1)

        def max_rows(H):
            b, h = divmod(H, NHEAD)
            mc = max_col
            bk = side_ring.take()
            for c in range(C):
                m = tr(bk.ap[0:SKM, c * P:(c + 1) * P], mc[:, c, :], ident[:, :], col_ok[H], *bk.free)
            last["mc_tr"] = m
            s = ACTE.do(lambda e: e.copy(q_st[b % 2][SK:SKM, h, :], bk.ap[SK:SKM, :]), m, g(("st_mm", b - 2)))
            bk.free = [s]
            rows_ok[H] = s

        pv_bank = {}

        def key_chunk(H, j):
            b, h = divmod(H, NHEAD)
            bk = st_ring.take()
            m = mm(bk.ap[:, :], k_st[b % 2][0:SKM, h, j * P:(j + 1) * P], q_st[b % 2][0:SKM, h, :], True, True,
                   rows_ok[H], *bk.free)
            last[("st_mm", b)] = m
            i, n = (H * C + j) % 2, (H * C + j) % PARTS
            ACTE.do(lambda e: e.activation(p_all[i][:, :], bk.ap[:, :], ACT.Exp, scale=SCALE), m, all_free[i])
            sh = ACTE.do(lambda e: e.activation(p_hi[n][:, :], bk.ap[:, :], ACT.Exp, scale=SCALE), hi_free[n])
            bk.free = [sh]
            return H, j, n, sh

        def key_rest(H, j, n, sh):
            i = (H * C + j) % 2
            line = POOL if i else DVE
            all_free[i] = sl = line.do(lambda e: e.tensor_tensor(
                p_lo[n][:, :], p_all[i][:, :], p_hi[n][:, :].bitcast(F32), ALU.subtract), sh, lo_free[n])
            return H, j, n, sh, sl

        def weighted(H, j, n, sh, sl):
            b, h = divmod(H, NHEAD)
            if j == 0:
                pv_bank[H] = pv_ring.take()
            pv = pv_bank[H]
            m = mm(pv.ap[0:VW, :], v_t[b % 2][:, j, h, :], p_hi[n][:, :], j == 0, False, sh, operands_of[b][2],
                   *(pv.free if j == 0 else []))
            hi_free[n] = m
            m = mm(pv.ap[0:VW, :], v_t[b % 2][:, j, h, :], p_lo[n][:, :], False, j == C - 1, sl)
            lo_free[n] = m
            last[("pv_mm", b)] = m
            if j == C - 1:
                heads_done.append(H)
                cp = ACTE.do(lambda e: e.copy(head_sb[H % 2][:, :], pv.ap[0:VW, :]), m, g(("fold_mm", H - 2)))
                pv.free = [cp]
                head_copied[H] = cp
                if h % 2 == 1:
                    tails.append(finish_pair(H // 2, head_copied[H - 1], cp))

        head_copied = {}

        def finish_pair(pair, *copied):
            b, h = divmod(2 * pair, NHEAD)
            half, n = h // HPH, pair % 2
            bk = side_ring.take()
            W2 = 2 * DQ
            for i in range(2):
                for c in range(C):
                    at = (i * C + c) * W2
                    m = mm(bk.ap[:, at:at + W2], head_sb[i][:, c * P:(c + 1) * P], fold[:, :], True, True, copied[i],
                           *bk.free)
                last[("fold_mm", 2 * pair + i)] = m
            turned = bk.ap[:, :].rearrange("p (i c w) -> p i c w", i=2, c=C)
            r = DVE.do(lambda e: e.reciprocal(sum_inv[:, :, :], turned[:, :, :, DQ]), m)
            for i in range(2):
                o = DVE.do(lambda e, i=i: e.tensor_tensor(
                    att_q[half][:, :, n, i * DQ:(i + 1) * DQ], turned[:, i, :, 0:DQ],
                    sum_inv[:, i, :].unsqueeze(2).to_broadcast([P, C, DQ]), ALU.mult), r, g(("att_tr", half)))
            bk.free = [o]
            yield
            if n == 1:
                bk = side_ring.take()
                for c in range(C):
                    m = tr(bk.ap[:, c * P:(c + 1) * P], att_q[half][:, c, :, :].rearrange("p n w -> p (n w)"),
                           ident[:, :], o, *bk.free)
                last[("att_tr", half)] = m
                xb = x_buf[b % NX]
                x3 = DVE.do(lambda e: e.tensor_tensor(xb[:, half, :], bk.ap[:, :], xb[:, half, :], ALU.add), m,
                            operands_of[b][3])
                bk.free = [x3]
                attended[(b, half)] = x3
            yield

        out_in = [arrivals(f"out_in{i}") for i in range(NX)]
        sent = [arrivals(f"sent{i}") for i in range(2)]
        sent_mark = [None, None]
        out_marks = [None] * NX

        now = {"chunk": 0}

        def side_turn():
            while now["chunk"] != 0:
                yield

        def dispatch(b):
            xb, rw, si = x_buf[b % NX], rows[b % 2], slot_i[b % 2]
            x3 = [attended[(b, i)] for i in range(HALF)]
            dst = out[b * HALF * P:(b + 1) * HALF * P, :].rearrange("(h p) t -> p h t", p=P)
            out_marks[b % NX] = om = SP.dma(lambda e: e.dma_start(dst, xb[:, :, :]), out_in[b % NX], *x3)
            w = norm_stats(halves(xb), row_stat4, row_mv4, row_rstd4, x3)
            yield
            yield
            xn_ok = norm_apply(halves(xb), halves(rw), row_mv4, row_rstd4, w, sent_mark[b % 2], filled[-1])
            x_free[b % NX] = [om, xn_ok]
            for k in range(HALF):
                no = DVE.do(lambda e, k=k: e.tensor_scalar(rw[:, k, T:T + 1].bitcast(I32), row_no[:, 0:1],
                                                           float((b * HALF + k) * P), None, ALU.add))
            yield
            for k in range(HALF):
                yield from side_turn()
                bk = side_ring.take()
                for c in range(C):
                    m = tr(bk.ap[:, c * P:(c + 1) * P], rw[:, k, c * P:(c + 1) * P], ident[:, :], xn_ok, *bk.free)
                t_ok = ACTE.do(lambda e, bk=bk, k=k: e.copy(x_t4[:, k, :, :],
                                                           bk.ap[:, :].rearrange("p (c q) -> p c q", c=C)),
                               m, g("route_mm"))
                bk.free = [t_ok]
                yield
            yield from side_turn()
            bk = side_ring.take()
            for k in range(HALF):
                for c in range(C):
                    m = mm(bk.ap[:, k * NEXP:(k + 1) * NEXP], x_t4[:, k, c, :], route_w[:, c, :], c == 0, c == C - 1,
                           t_ok, *bk.free)
            last["route_mm"] = m
            both = bk.ap[:, 0:HALF * NEXP].rearrange("p (k n) -> p k n", k=HALF)
            r = DVE.do(lambda e: e.tensor_reduce(r_max[:, :], both, X, ALU.max), m)
            r = DVE.do(lambda e: e.tensor_scalar(r_max[:, :], r_max[:, :], -1.0, None, ALU.mult), r)
            for k in range(HALF):
                s = ACTE.do(lambda e, bk=bk, k=k: e.activation(r_exp[:, k, :], bk.ap[:, k * NEXP:(k + 1) * NEXP],
                                                              ACT.Exp, bias=r_max[:, k:k + 1],
                                                              accum_out=r_sum[:, k:k + 1]), r)
            bk.free = [s]
            yield
            r = DVE.do(lambda e: e.reciprocal(r_inv[:, :], r_sum[:, :]), s)
            for k in range(HALF):
                pk = DVE.do(lambda e, k=k: e.tensor_scalar(r_exp[:, k, :], r_exp[:, k, :], r_inv[:, k:k + 1], None,
                                                           ALU.mult), r)
            for k in range(HALF):
                t8 = DVE.do(lambda e, k=k: e.max(top8[:, k, :], r_exp[:, k, :]), pk)
            for k in range(HALF):
                rp = DVE.do(lambda e, k=k: e.match_replace(out=repl[:, k, :], in_to_replace=top8[:, k, :],
                                                           in_values=r_exp[:, k, :], imm_value=-1.0), t8)
            s8 = DVE.do(lambda e: e.tensor_reduce(r_top[:, :], top8[:, :, :], X, ALU.add), t8)
            mk = DVE.do(lambda e: e.tensor_scalar(mask[:, :, :], repl[:, :, :], 0.0, None, ALU.is_lt), rp)
            r8 = DVE.do(lambda e: e.reciprocal(r_topi[:, :], r_top[:, :]), s8)
            for k in range(HALF):
                wt = DVE.do(lambda e, k=k: e.tensor_scalar(rw[:, k, T + 1:ROW], r_exp[:, k, :], r_topi[:, k:k + 1],
                                                           None, ALU.mult), r8)
            yield
            yield from side_turn()
            bk = side_ring.take()
            for k in range(HALF):
                dst_ap = bk.ap[:, k * NEXP:(k + 1) * NEXP]
                mm(dst_ap, below[:, :], mask[:, k, :], True, False, mk, *bk.free)
                for kk in range(k):
                    mm(dst_ap, ones[:, :], mask[:, kk, :], False, False)
                m = mm(dst_ap, ones[:, :], seen[:, :], False, True, g("seen"))
            for k in range(HALF):
                last["seen"] = DVE.do(lambda e, k=k: e.tensor_tensor(seen[:, :], seen[:, :], mask[:, k, :], ALU.add),
                                      m, last["seen"] if k else None)
            both2 = bk.ap[:, 0:HALF * NEXP].rearrange("p (k n) -> p k n", k=HALF)
            o1 = DVE.do(lambda e: e.tensor_scalar(over[:, :, :], both2, float(CAP), float(2 * NSLOT), ALU.is_ge,
                                                  ALU.mult), m)
            for k in range(HALF):
                o2 = DVE.do(lambda e, bk=bk, k=k: e.tensor_tensor(grid[:, k, :], bk.ap[:, k * NEXP:(k + 1) * NEXP],
                                                                  expert_off[:, :], ALU.add), m)
            bk.free = [o2]
            o = DVE.do(lambda e: e.tensor_tensor(grid[:, :, :], grid[:, :, :], over[:, :, :], ALU.add), o2, o1)
            o = DVE.do(lambda e: e.tensor_tensor(grid[:, :, :], grid[:, :, :], mask[:, :, :], ALU.mult), o)
            for k in range(HALF):
                o5 = DVE.do(lambda e, k=k: e.max(slot8[:, k, :], grid[:, k, :]), o)
            slots_ok = DVE.do(lambda e: e.tensor_scalar(si[:, :, :], slot8[:, :, :], -1.0, None, ALU.add), o5,
                              sent_mark[b % 2])
            yield
            for k in range(HALF):
                for n in range(TOPK):
                    mark = POOL.dma(lambda e, k=k, n=n: e.indirect_dma_start(
                        out=slots_dram, in_=rw[:, k, :], in_offset=None,
                        out_offset=bass.IndirectOffsetOnAxis(ap=si[:, k, n:n + 1].bitcast(U32), axis=0),
                        bounds_check=NSLOT - 1, oob_is_err=False),
                        sent[b % 2], slots_ok, wt, no, xn_ok, filled[-1])
                    yield
            sent_mark[b % 2] = mark

        def piece(gen):
            try:
                return "on" if next(gen) else "wait"
            except StopIteration:
                return "end"

        def run_all(gen):
            while piece(gen) != "end":
                pass

        AHEAD = 2
        SLOTS = NHEAD * C
        LOAD_AT, STATS_AT, PREPARE_AT, DISPATCH_AT = 8, 13, 23, 8
        load_batch(1)
        first_stats(0)
        run_all(prepare(0))
        first_stats(1)
        for H in range(AHEAD):
            for c in range(C):
                score_chunk(H, c)
            if H == 0:
                max_rows(0)
        preparing = prepare(1)
        upcoming = None
        dispatching = None
        whole, parts = [], []
        for n in range(B * SLOTS):
            b, s = divmod(n, SLOTS)
            H, j = divmod(n, C)
            if s == LOAD_AT and b + 2 < B:
                load_batch(b + 2)
            if s == STATS_AT and b + 2 < B:
                first_stats(b + 2)
            while b == 0 and len(filled) * SLOTS < NEXP * (s + 1):
                filled.append(fill(len(filled)))
            if s == SLOTS - AHEAD * C and b + 1 < B and b + 1 not in operands_of:
                run_all(preparing)
                preparing, upcoming = upcoming, None
            if whole:
                parts.append(key_rest(*whole.pop()))
            if len(parts) == PARTS:
                weighted(*parts.pop(0))
            whole.append(key_chunk(H, j))
            now["chunk"] = j
            if s == PREPARE_AT and b + 2 < B:
                upcoming = prepare(b + 2)
            if preparing is None and upcoming is not None:
                preparing, upcoming = upcoming, None
            while preparing is not None:
                played = piece(preparing)
                if played == "end":
                    preparing, upcoming = upcoming, None
                elif played == "wait":
                    break
            if H + AHEAD < B * NHEAD:
                score_chunk(H + AHEAD, j)
            if j >= 2 and tails and piece(tails[0]) == "end":
                tails.pop(0)
            if j == 1 and H + 1 < B * NHEAD:
                max_rows(H + 1)
            if s == DISPATCH_AT and b >= 1:
                if dispatching is not None:
                    run_all(dispatching)
                dispatching = dispatch(b - 1)
            if dispatching is not None:
                piece(dispatching)
        parts.append(key_rest(*whole.pop()))
        for part in parts:
            weighted(*part)
        for tail in tails:
            run_all(tail)
        if dispatching is not None:
            run_all(dispatching)
        now["chunk"] = 0
        run_all(dispatch(B - 1))

        end_a = [PE.last, ACTE.last, DVE.last, POOL.last]
        sent_all = [m for m in sent_mark if m is not None]
        small.close()
        NB = 5
        NW = 3
        W = lambda name, shape, dt=F32: sb(name, shape, dt)
        gu = [W(f"gate_up{i}", [P, C, 2 * INNER]) for i in range(NB)]
        dn = [W(f"down{i}", [IC, 2, T]) for i in range(NB)]
        xe = [W(f"x_slots{i}", [P, 2, ROW]) for i in range(NB)]
        gu_hi, gu_lo = ([W(f"gate_up_{part}{i}", [P, C, 2 * INNER], F32R) for i in range(NW)] for part in ("hi", "lo"))
        dn_hi, dn_lo = ([W(f"down_{part}{i}", [IC, 2, T], F32R) for i in range(NW)] for part in ("hi", "lo"))
        xt_hi, xt_lo = ([W(f"x_slots_t_{part}{i}", [P, C, P], F32R) for i in range(3)] for part in ("hi", "lo"))
        act_g = [W(f"silu{i}", [P, INNER]) for i in range(2)]
        hid = [W(f"hidden{i}", [P, INNER]) for i in range(2)]
        ht_hi, ht_lo = ([W(f"hidden_t_{part}{i}", [IC, 2, P], F32R) for i in range(2)] for part in ("hi", "lo"))
        ye = [W(f"y_slots{i}", [P, 2, T]) for i in range(2)]
        weights_of = [arrivals(f"expert_weights_in{i}") for i in range(NB)]
        rows_of = [arrivals(f"expert_rows_in{i}") for i in range(NB)]
        added = [arrivals(f"added{i}") for i in range(2)]
        xt_ring, gu_ring, ht_ring, y_ring = (Ring(banks[2 * i:2 * i + 2]) for i in range(4))
        w_mark, e_mark, y_mark, added_mark = {}, {}, {}, [None, None]
        xslot_read, gu_read, dn_read = {}, {}, {}
        SP.wait(*end_a, *[m for m in out_marks if m])

        def load_weights(e_):
            i = e_ % NB
            SP.dma(lambda e: e.dma_start(gu[i][:, :, :], a["gate_up"][e_]), weights_of[i], gu_read.get(e_ - NB))
            w_mark[e_] = SP.dma(lambda e: e.dma_start(dn[i][:, :, :], a["down"][e_]), weights_of[i],
                                dn_read.get(e_ - NB))

        def load_rows(e_):
            i = e_ % NB
            src = slots_dram[e_ * CAP:(e_ + 1) * CAP, :].rearrange("(c p) w -> p c w", p=P)
            e_mark[e_] = SP.dma(lambda e: e.dma_start(xe[i][:, :, :], src), rows_of[i], xslot_read.get(e_ - NB),
                                y_mark.get(e_ - NB))

        st = {}

        def turn(u):
            e_, s = divmod(u, 2)
            i = e_ % NB
            bk = xt_ring.take()
            for c in range(C):
                m = tr(bk.ap[:, c * P:(c + 1) * P], xe[i][:, s, c * P:(c + 1) * P], ident[:, :], e_mark[e_], *bk.free)
            st[("xt", u)] = split(bk, bk.ap[:, :].rearrange("p (c q) -> p c q", c=C), xt_hi[u % 3][:, :, :],
                                  xt_lo[u % 3][:, :, :], m, st.get(("gu_mm", u - 3)))

        def split(bk, src, hi_, lo_, m, free):
            h = ACTE.do(lambda e: e.copy(hi_, src), m, free)
            l = DVE.do(lambda e: e.tensor_tensor(lo_, src, hi_.bitcast(F32), ALU.subtract), h)
            bk.free = [l]
            return l

        rest_due = []

        def split_gate_up(e_, half):
            i, w = e_ % NB, e_ % NW
            cs = slice(half * C // 2, (half + 1) * C // 2)
            h = ACTE.do(lambda e: e.copy(gu_hi[w][:, cs, :], gu[i][:, cs, :]), w_mark[e_], gu_mm.get(e_ - NW))
            rest_due.append((e_, cs, h))

        def gate_up_rest(e_, cs, h):
            i, w = e_ % NB, e_ % NW
            gu_read[e_] = gu_ok[e_] = DVE.do(lambda e: e.tensor_tensor(
                gu_lo[w][:, cs, :], gu[i][:, cs, :], gu_hi[w][:, cs, :].bitcast(F32), ALU.subtract), h)

        def split_down(e_):
            i, w = e_ % NB, e_ % NW
            h = DVE.do(lambda e: e.tensor_copy(dn_hi[w][:, :, :], dn[i][:, :, :]), w_mark[e_], dn_mm.get(e_ - NW))
            dn_read[e_] = dn_ok[e_] = POOL.do(lambda e: e.tensor_tensor(
                dn_lo[w][:, :, :], dn[i][:, :, :], dn_hi[w][:, :, :].bitcast(F32), ALU.subtract), h)

        gu_ok, dn_ok, gu_mm, dn_mm = {}, {}, {}, {}

        def up(u):
            e_, s = divmod(u, 2)
            i = e_ % NB
            bk = gu_ring.take()
            w = e_ % NW
            pairs = [(x_, w_, c) for c in range(C) for x_, w_ in ((xt_hi, gu_hi), (xt_hi, gu_lo), (xt_lo, gu_hi))]
            for n, (x_, w_, c) in enumerate(pairs):
                m = mm(bk.ap[:, 0:2 * INNER], x_[u % 3][:, c, :], w_[w][:, c, :], n == 0, n == len(pairs) - 1,
                       st[("xt", u)], gu_ok[e_], *bk.free)
            st[("gu_mm", u)] = gu_mm[e_] = m
            o = ACTE.do(lambda e: e.activation(act_g[u % 2][:, :], bk.ap[:, 0:INNER], ACT.Silu), m,
                        st.get(("hid", u - 2)))
            h = DVE.do(lambda e: e.tensor_tensor(hid[u % 2][:, :], bk.ap[:, INNER:2 * INNER], act_g[u % 2][:, :],
                                                 ALU.mult), o, st.get(("hid_tr", u - 2)))
            bk.free = [h]
            st[("hid", u)] = h

        def turn_hidden(u):
            bk = ht_ring.take()
            for n in range(2):
                m = tr(bk.ap[0:IC, n * P:(n + 1) * P], hid[u % 2][:, n * IC:(n + 1) * IC], ident[:, :], st[("hid", u)],
                       *bk.free)
            st[("hid_tr", u)] = m
            st[("ht", u)] = split(bk, bk.ap[0:IC, 0:2 * P].rearrange("p (n q) -> p n q", n=2), ht_hi[u % 2][:, :, :],
                                  ht_lo[u % 2][:, :, :], m, st.get(("y_mm", u - 2)))

        def down(u):
            e_, s = divmod(u, 2)
            i = e_ % NB
            bk = y_ring.take()
            w = e_ % NW
            pairs = [(h_, w_, c) for c in range(2) for h_, w_ in ((ht_hi, dn_hi), (ht_hi, dn_lo), (ht_lo, dn_hi))]
            for n, (h_, w_, c) in enumerate(pairs):
                m = mm(bk.ap[:, :], h_[u % 2][:, c, :], w_[w][:, c, :], n == 0, n == len(pairs) - 1, st[("ht", u)],
                       dn_ok[e_], *bk.free)
            st[("y_mm", u)] = dn_mm[e_] = m
            o = ACTE.do(lambda e: e.activation(ye[e_ % 2][:, s, :], bk.ap[:, :], ACT.Copy,
                                               scale=xe[i][:, s, T + 1 + e_:T + 2 + e_]), m, added_mark[e_ % 2])
            bk.free = [o]
            st[("y", u)] = xslot_read[e_] = o
            if s == 1:
                prev = y_mark.get(e_ - 1)
                for q in range(2):
                    y_mark[e_] = POOL.dma(lambda e, q=q: e.indirect_dma_start(
                        out=out, out_offset=bass.IndirectOffsetOnAxis(ap=xe[i][:, q, T:T + 1].bitcast(U32), axis=0),
                        in_=ye[e_ % 2][:, q, :], in_offset=None, compute_op=ALU.add),
                        added[e_ % 2], o, st[("y", u - 1)], prev, e_mark[e_])
                added_mark[e_ % 2] = y_mark[e_]

        U = 2 * NEXP
        load_weights(0)
        SP.wait(*sent_all)
        for e_ in range(min(NB - 2, NEXP)):
            load_rows(e_)
            if e_ + 1 < NEXP:
                load_weights(e_ + 1)
        for line in (DVE, ACTE, PE, POOL):
            line.wait(*end_a)
        for t in range(-6, U):
            if t >= 0 and t % 2 == 0 and t // 2 + NB - 1 < NEXP:
                load_weights(t // 2 + NB - 1)
            if t >= 0 and t % 2 == 0 and t // 2 + NB - 2 < NEXP:
                load_rows(t // 2 + NB - 2)
            if 0 <= t + 3 < U:
                turn(t + 3)
            if 0 <= t + 2 < U:
                up(t + 2)
            if 0 <= t + 1 < U:
                turn_hidden(t + 1)
            if t >= 0:
                down(t)
            for due in rest_due:
                gate_up_rest(*due)
            rest_due.clear()
            if (t + 6) // 2 < NEXP:
                split_gate_up((t + 6) // 2, t % 2)
            if t % 2 == 0 and 0 <= (t + 4) // 2 < NEXP:
                split_down((t + 4) // 2)
        SP.wait(*[m for m in added_mark if m], *[m for m in out_marks if m], filled[-1], *sent_all)

        lines = (("tensor", PE), ("vector", DVE), ("scalar", ACTE), ("gpsimd", POOL), ("sync", SP))
        for _, line in lines:
            line.number()
        block = stack.enter_context(nc.Block())

        @block.tensor
        def _(e):
            PE.play(e)

        @block.vector
        def _(e):
            DVE.play(e)

        @block.scalar
        def _(e):
            ACTE.play(e)

        @block.gpsimd
        def _(e):
            POOL.play(e)

        @block.sync
        def _(e):
            SP.play(e)


def kernel(x, ctx_2048, L0_xattn_theta_w, L0_xattn_theta_b, L0_xattn_phi_w, L0_xattn_phi_b, L0_xattn_g_w,
           L0_xattn_g_b, L0_xattn_ln_gamma, L0_xattn_ln_beta, L0_xattn_out_w, L0_xattn_out_b, L0_ffn_W_base,
           L0_ffn_b_base, L0_ffn_W_router, L0_ffn_A_w, L0_ffn_B_w, L1_xattn_gamma, L1_ffn_router_weight,
           L1_ffn_gate_proj, L1_ffn_up_proj, L1_ffn_down_proj):
    import concourse.bacc as _bacc
    from concourse.bass_utils import run_bass_kernel_spmd as _run

    n = np.asarray
    B, rows, T = x.shape
    HALF = rows // P
    NE, NRANK, _ = L0_ffn_A_w.shape
    NEXP, D, INNER = L1_ffn_gate_proj.shape
    dims = dict(B=B, HALF=HALF, T=T, L=L0_xattn_theta_w.shape[0], NHEAD=8, DQ=rows // 8, NE=NE, NRANK=NRANK,
                NEXP=NEXP, CAP=2 * (2 * 512 * 8) // NEXP, TOPK=8, INNER=INNER, LORA_SCALE=16.0 / NRANK)
    CAP = dims["CAP"]
    gate_up = np.concatenate([n(L1_ffn_gate_proj), n(L1_ffn_up_proj)], axis=2)
    gate_up = gate_up.reshape(NEXP, D // P, P, 2 * INNER).transpose(0, 2, 1, 3)
    down = n(L1_ffn_down_proj).reshape(NEXP, 2, INNER // 2, D).transpose(0, 2, 1, 3)
    arrays = {
        "x": n(x), "ctx": n(ctx_2048),
        "theta_wT": n(L0_xattn_theta_w).T, "phi_wT": n(L0_xattn_phi_w).T, "g_wT": n(L0_xattn_g_w).T,
        "lat_b": np.stack([n(L0_xattn_theta_b), n(L0_xattn_phi_b), n(L0_xattn_g_b)], axis=1),
        "ln_gamma": n(L0_xattn_ln_gamma), "ln_beta": n(L0_xattn_ln_beta),
        "out_wT": n(L0_xattn_out_w).T, "out_b": n(L0_xattn_out_b).reshape(HALF, P).T,
        "base_wT": n(L0_ffn_W_base).T,
        "lora_in": np.concatenate([n(L0_ffn_W_router), n(L0_ffn_A_w).reshape(NE * NRANK, T)], axis=0).T,
        "lora_out": np.concatenate([n(L0_ffn_B_w).transpose(0, 2, 1).reshape(NE * NRANK, T),
                                    n(L0_ffn_b_base).reshape(1, T)], axis=0),
        "route_w": n(L1_ffn_router_weight),
        "gamma1": np.broadcast_to(n(L1_xattn_gamma).reshape(1, 1), (P, 1)),
        "gate_up": gate_up, "down": down,
    }
    arrays = {f"in_{k}": np.ascontiguousarray(v) for k, v in arrays.items()}
    nc = _bacc.Bacc("TRN2", target_bir_lowering=False, num_devices=1)
    aps = {k[3:]: nc.dram_tensor(k, v.shape, mybir.dt.from_np(v.dtype), kind="ExternalInput").ap()
           for k, v in arrays.items()}
    out = nc.dram_tensor("out_rows", (B * rows + CAP, T), F32, kind="ExternalOutput").ap()
    slots = nc.dram_tensor("slot_rows", (NEXP * CAP, T + 1 + NEXP), F32, kind="Internal").ap()
    build(nc, aps, out, slots, dims)
    r = _run(nc, [arrays], core_ids=[0])
    return r.results[0]["out_rows"][:B * rows].reshape(B, rows, T)
```
